# Optimizing a Trainium2 kernel written in Bass

```python
import numpy as np
import jax
import jax.numpy as jnp

def _softmax(x, axis=-1):
    return jax.nn.softmax(x, axis=axis)

def _gelu(x):
    return jax.nn.gelu(x, approximate=True)

def _silu(x):
    return jax.nn.silu(x)

def _sigmoid(x):
    return jax.nn.sigmoid(x)

def _layernorm(x, axis=-1, eps=1e-05):
    m = jnp.mean(x, axis=axis, keepdims=True)
    v = jnp.var(x, axis=axis, keepdims=True)
    return (x - m) / jnp.sqrt(v + eps)

def _scatter_add(tgt, idx, src, axis=0):
    return tgt.at[idx].add(src)

def _segment_sum(src, seg, n):
    return jax.ops.segment_sum(src, seg, n)
kernel_name = 'mk_cond_resid_d2_seqx_r4_849108'

def setup_inputs(seed: int=0):
    np.random.seed(seed)
    _w = jnp.asarray

    def _rec_inputs():
        import jax
        import jax.numpy as jnp
        _rk = jax.random.key(seed)
        x = -0.0003929 + 0.9999 * jax.random.normal(jax.random.fold_in(_rk, 1), (64, 64, 1024), jnp.float32)
        _lenS = 64 - jax.random.randint(jax.random.fold_in(_rk, 7), (64,), 0, max(1, 64 // 4) + 1, jnp.int32)
        _lenS2 = 64 - jax.random.randint(jax.random.fold_in(_rk, 8), (64,), 0, max(1, 64 // 4) + 1, jnp.int32)
        itok_B_78_3631 = jax.random.randint(jax.random.fold_in(_rk, 11), (64,), 78, 908, jnp.int32)
        itok_B_0_7 = jax.random.randint(jax.random.fold_in(_rk, 12), (64,), 0, 8, jnp.int32)
        itok_B_2182_4065 = jax.random.randint(jax.random.fold_in(_rk, 14), (64,), 2182, 4066, jnp.int32)
        return (x, itok_B_78_3631, itok_B_0_7, itok_B_2182_4065, _lenS)
    x, itok_B_78_3631, itok_B_0_7, itok_B_2182_4065, _lenS = _rec_inputs()

    def _L0_cond_setup():
        import math
        import jax, jax.numpy as jnp
        import numpy as np
        B, H, N, L = (16, 64, 64, 1024)
        DT_MIN, DT_MAX = (0.001, 0.1)

        def _get_kernel(log_dt, C, log_A_real, A_imag, length):
            dt = jnp.exp(log_dt)
            Cc = C[..., 0] + 1j * C[..., 1]
            A = -jnp.exp(log_A_real) + 1j * A_imag
            dtA = A * dt[:, None]
            Ct = Cc * (jnp.exp(dtA) - 1.0) / A
            P = dtA[:, :, None] * jnp.arange(length, dtype=jnp.float32)
            K = 2.0 * jnp.einsum('hn,hnl->hl', Ct, jnp.exp(P)).real
            return K
        key = jax.random.key(seed)
        ks = jax.random.split(key, 5)
        u = jax.random.normal(ks[0], (B, H, L), dtype=jnp.float32)
        log_dt = jax.random.uniform(ks[1], (H,), dtype=jnp.float32) * (math.log(DT_MAX) - math.log(DT_MIN)) + math.log(DT_MIN)
        C = jax.random.normal(ks[2], (H, N, 2), dtype=jnp.float32)
        log_A_real = jnp.log(0.5 * jnp.ones((H, N), dtype=jnp.float32))
        A_imag = math.pi * jnp.broadcast_to(jnp.arange(N, dtype=jnp.float32), (H, N))
        D = jax.random.normal(ks[3], (H,), dtype=jnp.float32)
        length = jax.random.randint(ks[4], (B,), 1, L + 1, dtype=jnp.int32)
        return {'u': u, 'log_dt': log_dt, 'C': C, 'log_A_real': log_A_real, 'A_imag': A_imag, 'D': D, 'length': length}
    _L0_cond_all = _L0_cond_setup()
    _L0_cond_in = {k: v for k, v in _L0_cond_all.items() if k in ('log_dt', 'C', 'log_A_real', 'A_imag', 'D')}
    del _L0_cond_all

    def _L1_cond_setup():
        import jax, jax.numpy as jnp
        import numpy as np
        SESSION_CHANNELS = [128, 160, 192, 224, 240, 248, 252, 64]
        N_SESS = len(SESSION_CHANNELS)
        B, MAX_C, MAX_T = (16, 64, 1024)
        HID, N_SRC = (128, 64)
        key = jax.random.key(seed)
        ks = jax.random.split(key, 7)
        session_ids = jax.random.randint(ks[0], (B,), 0, N_SESS)
        chan_table = jnp.asarray(SESSION_CHANNELS)
        channel_counts = chan_table[session_ids]
        seq_lens = jax.random.randint(ks[1], (B,), MAX_T // 2, MAX_T + 1)
        x = jax.random.normal(ks[2], (B, MAX_C, MAX_T), jnp.float32)
        cmask = (jnp.arange(MAX_C)[None, :] < channel_counts[:, None]).astype(x.dtype)
        tmask = (jnp.arange(MAX_T)[None, :] < seq_lens[:, None]).astype(x.dtype)
        x = x * cmask[:, :, None] * tmask[:, None, :]
        lim1 = 1.0 / np.sqrt(MAX_C)
        W_sess = jax.random.uniform(ks[3], (N_SESS, MAX_C, HID), jnp.float32, -lim1, lim1)
        b_sess = jax.random.uniform(ks[4], (N_SESS, HID), jnp.float32, -lim1, lim1)
        lim2 = 1.0 / np.sqrt(HID)
        W2 = jax.random.uniform(ks[5], (HID, N_SRC), jnp.float32, -lim2, lim2)
        b2 = jax.random.uniform(ks[6], (N_SRC,), jnp.float32, -lim2, lim2)
        return dict(x=x, session_ids=session_ids, channel_counts=channel_counts, seq_lens=seq_lens, W_sess=W_sess, b_sess=b_sess, W2=W2, b2=b2)
    _L1_cond_all = _L1_cond_setup()
    _L1_cond_in = {k: v for k, v in _L1_cond_all.items() if k in ('W_sess', 'b_sess', 'W2', 'b2')}
    del _L1_cond_all
    return {'x': x, 'itok_B_78_3631': itok_B_78_3631, 'itok_B_0_7': itok_B_0_7, 'itok_B_2182_4065': itok_B_2182_4065, '_lenS': _lenS, 'L0_cond_log_dt': _L0_cond_in['log_dt'], 'L0_cond_C': _L0_cond_in['C'], 'L0_cond_log_A_real': _L0_cond_in['log_A_real'], 'L0_cond_A_imag': _L0_cond_in['A_imag'], 'L0_cond_D': _L0_cond_in['D'], 'L1_cond_W_sess': _L1_cond_in['W_sess'], 'L1_cond_b_sess': _L1_cond_in['b_sess'], 'L1_cond_W2': _L1_cond_in['W2'], 'L1_cond_b2': _L1_cond_in['b2']}

def reference(x, itok_B_78_3631, itok_B_0_7, itok_B_2182_4065, _lenS, L0_cond_log_dt, L0_cond_C, L0_cond_log_A_real, L0_cond_A_imag, L0_cond_D, L1_cond_W_sess, L1_cond_b_sess, L1_cond_W2, L1_cond_b2):
    import jax
    import jax.numpy as jnp

    def _L0_cond_ref(u, log_dt, C, log_A_real, A_imag, D, length):
        import math
        import jax, jax.numpy as jnp
        import numpy as np
        B, H, N, L = (16, 64, 64, 1024)
        DT_MIN, DT_MAX = (0.001, 0.1)

        def _get_kernel(log_dt, C, log_A_real, A_imag, length):
            dt = jnp.exp(log_dt)
            Cc = C[..., 0] + 1j * C[..., 1]
            A = -jnp.exp(log_A_real) + 1j * A_imag
            dtA = A * dt[:, None]
            Ct = Cc * (jnp.exp(dtA) - 1.0) / A
            P = dtA[:, :, None] * jnp.arange(length, dtype=jnp.float32)
            K = 2.0 * jnp.einsum('hn,hnl->hl', Ct, jnp.exp(P)).real
            return K
        Bq, Hq, Lq = u.shape
        K = _get_kernel(log_dt, C, log_A_real, A_imag, Lq)
        n = 2 * Lq
        kf = jnp.fft.rfft(K, n=n)
        uf = jnp.fft.rfft(u, n=n)
        y = jnp.fft.irfft(uf * kf[None], n=n)[..., :Lq]
        y = y + u * D[:, None]
        mask = (jnp.arange(Lq)[None, :] < length[:, None]).astype(u.dtype)
        return y * mask[:, None, :]

    def _L1_cond_ref(x, session_ids, channel_counts, seq_lens, W_sess, b_sess, W2, b2):
        import jax, jax.numpy as jnp
        import numpy as np
        SESSION_CHANNELS = [128, 160, 192, 224, 240, 248, 252, 64]
        N_SESS = len(SESSION_CHANNELS)
        B, MAX_C, MAX_T = (16, 64, 1024)
        HID, N_SRC = (128, 64)
        cmask = (jnp.arange(x.shape[1])[None, :] < channel_counts[:, None]).astype(x.dtype)
        xm = x * cmask[:, :, None]
        W = W_sess[session_ids]
        b = b_sess[session_ids]
        h = jnp.einsum('bct,bch->bht', xm, W) + b[:, :, None]
        h = jax.nn.gelu(h, approximate=False)
        out = jnp.einsum('bht,hs->bst', h, W2) + b2[None, :, None]
        tmask = (jnp.arange(x.shape[2])[None, :] < seq_lens[:, None]).astype(x.dtype)
        return out * tmask[:, None, :]
    x = x + _L0_cond_ref(x, L0_cond_log_dt, L0_cond_C, L0_cond_log_A_real, L0_cond_A_imag, L0_cond_D, itok_B_78_3631)
    x = x + _L1_cond_ref(x, itok_B_0_7, _lenS, itok_B_2182_4065, L1_cond_W_sess, L1_cond_b_sess, L1_cond_W2, L1_cond_b2)
    return x

_drawn_inputs = setup_inputs


def setup_inputs(seed=0):
    import zlib

    import numpy as np

    out = dict(_drawn_inputs(seed))
    spreads = {'L0_cond_log_A_real': (-0.6931471824645996, 0.2)}
    factors = {'L1_cond_b_sess': 3.381}
    for name, (base, spread) in spreads.items():
        noise = np.random.default_rng([zlib.crc32(name.encode()), seed]).standard_normal(out[name].shape)
        drawn = base * np.exp(spread * noise) if base else spread * noise
        out[name] = jnp.asarray(drawn.astype(out[name].dtype))
    for name, factor in factors.items():
        out[name] = (out[name] * factor).astype(out[name].dtype)
    return out
```

```python
import math
from contextlib import ExitStack

import concourse.bass as bass
from concourse import mybir

F32 = mybir.dt.float32
F32R = mybir.dt.float32r
I32 = mybir.dt.int32
ALU = mybir.AluOpType
ACT = mybir.ActivationFunctionType

B, C, T = 64, 64, 1024
N = 64
HID, SESS = 128, 8
P = 128
CH = T // P
PAIRS = C // 2
HALF = T // 2
RAD = 32
LAG0 = 3
KPAD = T + P
QUAD = 4
GROUPS = 4
GC = C // GROUPS
MAGIC = 1.5 * 2.0 ** 23
TURN = 6.283185
INV_TURN = 1.0 / (2.0 * math.pi)


def need(eng, sem, value):
    if isinstance(value, int) and value <= 0:
        return
    eng.wait_ge(sem, value)


def build_program(nc, x, len1, sid, len2, chans, log_dt, cc, log_a, a_imag, dskip, w_sess, b_sess, w2, b2, out):
    kr = nc.dram_tensor("kr", (C, KPAD), F32, kind="Internal").ap()
    x_rows = x.rearrange("b c t -> (b c) t")
    out_rows = out.rearrange("b c t -> (b c) t")
    toeplitz = bass.AP(kr.tensor, 0, [[KPAD, C], [1, P], [1, T]])

    ctx = ExitStack()
    early = ExitStack()
    late = ExitStack()
    with ctx:
        def sb(name, shape, dt=F32, where=ctx):
            return where.enter_context(nc.sbuf_tensor(name, shape, dt))

        def sem(name):
            return ctx.enter_context(nc.semaphore(name))

        ident = sb("ident", [P, P])
        ones = sb("ones", [P, P])
        time_i = sb("time_i", [P, CH], I32)
        time_rev = sb("time_rev", [P, CH])
        mask1 = sb("mask1", [P, CH, B])
        row_i = sb("row_i", [P, T], I32)
        row_t = sb("row_t", [P, T])
        chan_i = sb("chan_i", [P, 1], I32)
        chan_of = sb("chan_of", [P, 1])
        ints = sb("ints", [P, 4, B], I32)
        ints_f = sb("ints_f", [P, 4, B])
        len2_p = sb("len2_p", [P, PAIRS])
        cmask = sb("cmask", [P, PAIRS])
        sess_i = sb("sess_i", [SESS, 1], I32)
        sess_of = sb("sess_of", [SESS, 1])
        onehot = sb("onehot", [SESS, B])
        bs = sb("bs", [SESS, HID])
        bias_t = sb("bias_t", [P, B])
        w2_s = sb("w2_s", [HID, C])
        b2_col = sb("b2_col", [P, 1])

        xin = sb("xin", [P, 2, T])
        la = sb("la", [C, N], where=early)
        ai = sb("ai", [C, N], where=early)
        ccs = sb("ccs", [C, N, 2], where=early)
        ld = sb("ld", [C, 1], where=early)
        dt_c = sb("dt_c", [C, 1], where=early)
        small = sb("small", [C, 20, N], where=early)
        stack = sb("stack", [C, 4, P], where=early)
        par = sb("par", [P, 4, C], where=early)
        exps_i = sb("exps_i", [P, 2, RAD], I32, where=early)
        exps = sb("exps", [P, 2, RAD], where=early)
        phase = sb("phase", [P, 4], where=early)
        mag1 = sb("mag1", [P, C, RAD], where=early)
        mag2 = sb("mag2", [P, C, RAD], where=early)
        turns = sb("turns", [P, 2, GC, RAD], where=early)
        nearest = sb("nearest", [P, 3, GC, RAD], where=early)
        wave = sb("wave", [P, 3, GC, RAD], where=early)
        e1 = sb("e1", [P, 2, GC, RAD], where=early)
        e2 = sb("e2", [P, 2, GC, RAD], where=early)
        dplace = sb("dplace", [P, C // QUAD, RAD], where=early)
        krow = sb("krow", [P, GROUPS, GC // QUAD, RAD], where=early)
        zrow = sb("zrow", [C, P], where=early)
        early.close()
        y = sb("y", [P, PAIRS, CH, 2, C])
        wf = sb("wf", [P, 2, T], where=late)
        wh = sb("wh", [P, 2, T], F32R, where=late)
        wl = sb("wl", [P, 2, T], F32R, where=late)
        xh = sb("xh", [P, 2, 2, LAG0 + CH, B], F32R, where=late)
        xl = sb("xl", [P, 2, 2, LAG0 + CH, B], F32R, where=late)
        late.close()
        ys = sb("ys", [P, 2, CH, P])
        xc = sb("xc", [P, 2, T])
        xch = sb("xch", [P, 2, HALF], F32R)
        xcl = sb("xcl", [P, 2, HALF], F32R)
        hid = sb("hid", [P, 2, 2, HALF])
        tmask = sb("tmask", [P, 2, HALF])
        z = sb("z", [P, 2, T])
        wg = sb("wg", [P, 2, HID])
        wbh = sb("wbh", [P, 2, 2, HID], F32R)
        wbl = sb("wbl", [P, 2, 2, HID], F32R)

        ps_t = ctx.enter_context(nc.psum_tensor("ps_t", [P, 2, 512], F32))
        ps_y = ctx.enter_context(nc.psum_tensor("ps_y", [P, 2, 512], F32))
        ps_h = ctx.enter_context(nc.psum_tensor("ps_h", [P, 2, 2, 512], F32))

        in_small = sem("in_small")
        in_ints = sem("in_ints")
        in_late = sem("in_late")
        in_d = sem("in_d")
        ident_done = sem("ident_done")
        iota_done = sem("iota_done")
        d_zero = sem("d_zero")
        chain = sem("chain")
        dt_done = sem("dt_done")
        red_half = sem("red_half")
        sin_half = sem("sin_half")
        stack_done = sem("stack_done")
        par_t = sem("par_t")
        mag_arg = sem("mag_arg")
        mag_done = sem("mag_done")
        wave_arg = sem("wave_arg")
        wave_done = sem("wave_done")
        e_done = sem("e_done")
        k_done = sem("k_done")
        krow_done = sem("krow_done")
        k_pad = sem("k_pad")
        k_stored = [sem(f"k_stored{g}") for g in range(GROUPS)]
        onehot_done = sem("onehot_done")
        bias_mm = sem("bias_mm")
        tables_done = sem("tables_done")
        x_zero = sem("x_zero")
        x_loaded = [sem(f"x_loaded{n}") for n in range(2)]
        w_loaded = [sem(f"w_loaded{n}") for n in range(2)]
        xt_done = sem("xt_done")
        xh_done = sem("xh_done")
        xl_done = sem("xl_done")
        wh_done = sem("wh_done")
        wl_done = sem("wl_done")
        conv_done = sem("conv_done")
        y_done = sem("y_done")
        xn_loaded = [sem(f"xn_loaded{n}") for n in range(2)]
        ys_loaded = [sem(f"ys_loaded{n}") for n in range(2)]
        wg_loaded = [sem(f"wg_loaded{n}") for n in range(2)]
        wb_zero = sem("wb_zero")
        wbh_done = sem("wbh_done")
        wbl_done = sem("wbl_done")
        t2_done = sem("t2_done")
        xc_done = sem("xc_done")
        xch_done = sem("xch_done")
        xcl_done = sem("xcl_done")
        mm1_done = sem("mm1_done")
        hid_done = sem("hid_done")
        mm2_done = sem("mm2_done")
        tmask_done = sem("tmask_done")
        z_done = sem("z_done")
        out_done = sem("out_done")
        stored = [sem(f"stored{n}") for n in range(2)]

        block = ctx.enter_context(nc.Block())

        STEPS = 2 * PAIRS

        def steps_of(eng, step):
            for k in (2, 3):
                step(-1, k)
            for k in range(4):
                step(0, k)
            with eng.Fori(1, STEPS // 4 - 1) as i:
                for k in range(4):
                    step(i, k)
            for k in range(4):
                step(STEPS // 4 - 1, k)

        def exists(i, k):
            return not isinstance(i, int) or 0 <= 4 * i + k < STEPS

        @block.sync
        def _(sp):
            sp.dma_start(ld[:], log_dt.rearrange("(h a) -> h a", a=1)).then_inc(in_small, 16)
            sp.dma_start(la[:], log_a).then_inc(in_small, 16)
            sp.dma_start(ai[:], a_imag).then_inc(in_small, 16)
            sp.dma_start(ccs[:], cc).then_inc(in_small, 16)
            for n, v in enumerate((len1, len2, chans, sid)):
                sp.dma_start(ints[:, n, :], bass.AP(v.tensor, 0, [[0, P], [1, B]])).then_inc(in_ints, 16)

            def load_x(i, m):
                need(sp, xt_done, i * 2 + (m - 1))
                for h in range(2):
                    src = x[:, bass.ds(i * 4 + (2 * m + h), 1), :].rearrange("b c t -> (b c) t")
                    sp.dma_start(xin[h * B:(h + 1) * B, m % 2, :], src).then_inc(x_loaded[m % 2], 16)

            def load_w(i, k):
                need(sp, wl_done, i * 4 + (k - 1))
                src = toeplitz[bass.ds(i * 4 + k, 1)].rearrange("h s c -> (h s) c")
                sp.dma_start(wf[:, k % 2, :], src).then_inc(w_loaded[k % 2], 16)

            load_x(0, 0)
            load_x(0, 1)
            sp.wait_ge(d_zero, 1)
            for q in range(QUAD):
                sp.dma_start(dplace[RAD * q + RAD - 1:RAD * q + RAD, :, RAD - 1:RAD],
                             bass.AP(dskip.tensor, q, [[C, 1], [QUAD, C // QUAD], [1, 1]]),
                             allow_slow_non_contiguous=True).then_inc(in_d, 16)
            sp.dma_start(kr[:, T:KPAD], zrow[:]).then_inc(k_pad, 16)
            sp.dma_start(bs[:], b_sess).then_inc(in_late, 16)
            sp.dma_start(w2_s[:], w2).then_inc(in_late, 16)
            for n in range(2):
                sp.dma_start(b2_col[n * C:(n + 1) * C, :], b2.rearrange("(s a) -> s a", a=1)).then_inc(in_late, 16)
            for g in range(GROUPS):
                sp.wait_ge(krow_done, g + 1)
                for q in range(QUAD):
                    dst = bass.AP(kr.tensor, (GC * g + q) * KPAD, [[RAD, RAD], [QUAD * KPAD, GC // QUAD], [1, RAD]])
                    sp.dma_start(dst, krow[RAD * q:RAD * (q + 1), g, :, :]).then_inc(k_stored[g], 16)
            sp.wait_ge(k_pad, 16)
            sp.wait_ge(k_stored[0], 16 * QUAD)
            load_w(0, 0)
            load_w(0, 1)
            for g in range(1, GROUPS):
                sp.wait_ge(k_stored[g], 16 * QUAD)

            def loads1(i):
                for m in range(2):
                    if not isinstance(i, int) or 4 * i + 2 * m + 2 < C:
                        load_w(i, 2 * m + 2)
                    if not isinstance(i, int) or 4 * i + 2 * m + 4 < C:
                        load_x(i, m + 2)
                    if not isinstance(i, int) or 4 * i + 2 * m + 3 < C:
                        load_w(i, 2 * m + 3)

            loads1(0)
            with sp.Fori(1, C // 4 - 1) as i:
                loads1(i)
            loads1(C // 4 - 1)

            def load_pair(i, m):
                need(sp, t2_done, i * 4 + (2 * m - 2))
                q = i * 2 + m
                sp.dma_start(ys[:, m % 2, :, :].rearrange("p i n -> p (i n)"),
                             y[:, bass.ds(q, 1), :, :, :].rearrange("p q i b c -> p (q i b c)")
                             ).then_inc(ys_loaded[m % 2], 16)
                need(sp, xc_done, i * 4 + (2 * m - 2))
                sp.dma_start(xin[:, m % 2, :], x_rows[bass.ds(i * (2 * P) + m * P, P), :]
                             ).then_inc(xn_loaded[m % 2], 16)
                need(sp, wbl_done, i * 2 + (m - 1))
                for b in range(2):
                    s = sp.value_load(ints[0:1, 3, bass.ds(i * 4 + (2 * m + b), 1)], min_val=0, max_val=SESS - 1)
                    sp.dma_start(wg[b * C:(b + 1) * C, m % 2, :],
                                 w_sess[bass.ds(s, 1)].rearrange("s c n -> (s c) n")).then_inc(wg_loaded[m % 2], 16)

            def store_pair(i, m):
                sp.wait_ge(out_done, i * 4 + (2 * m + 2))
                sp.dma_start(out_rows[bass.ds(i * (2 * P) + m * P, P), :], z[:, m % 2, :]
                             ).then_inc(stored[m % 2], 16)

            sp.wait_ge(xt_done, PAIRS)
            sp.wait_ge(y_done, C)
            load_pair(0, 0)
            load_pair(0, 1)

            def moves2(i):
                for m in range(2):
                    if not isinstance(i, int) or 2 * i + m + 2 < PAIRS:
                        load_pair(i, m + 2)
                    if not isinstance(i, int) or 2 * i + m > 0:
                        store_pair(i - (1 - m), 1 - m)

            moves2(0)
            with sp.Fori(1, PAIRS // 2 - 1) as i:
                moves2(i)
            moves2(PAIRS // 2 - 1)
            store_pair(PAIRS // 2 - 1, 1)
            for n in range(2):
                sp.wait_ge(stored[n], 16 * (PAIRS // 2))

        @block.gpsimd
        def _(pool):
            nc.gpsimd.memset(dplace[:], 0.0)
            nc.gpsimd.memset(zrow[:], 0.0).then_inc(d_zero, 1)
            nc.gpsimd.memset(ones[:], 1.0).then_inc(ident_done, 1)
            pool.wait_ge(ident_done, 1)
            nc.gpsimd.affine_select(out=ident[:], in_=ones[:], compare_op=ALU.is_equal, fill=0.0, base=0,
                                    pattern=[[-1, P]], channel_multiplier=1).then_inc(ident_done, 1)
            nc.gpsimd.iota(exps_i[:, 0, :], pattern=[[-1, RAD]], base=RAD - 1, channel_multiplier=0).then_inc(iota_done, 1)
            nc.gpsimd.iota(exps_i[:, 1, :], pattern=[[-RAD, RAD]], base=RAD * (RAD - 1),
                           channel_multiplier=0).then_inc(iota_done, 1)
            nc.gpsimd.iota(time_i[:], pattern=[[P, CH]], base=P - 1, channel_multiplier=-1).then_inc(iota_done, 1)
            nc.gpsimd.iota(row_i[:], pattern=[[1, T]], base=0, channel_multiplier=0).then_inc(iota_done, 1)
            for n in range(2):
                pool.wait_ge(iota_done, 4 + n)
                nc.gpsimd.iota(chan_i[n * C:(n + 1) * C, :], pattern=[[0, 1]], base=0,
                               channel_multiplier=1).then_inc(iota_done, 1)
            pool.wait_ge(iota_done, 6)
            nc.gpsimd.iota(sess_i[:], pattern=[[0, 1]], base=0, channel_multiplier=1).then_inc(iota_done, 1)

            def step(i, k):
                if not exists(i, k):
                    return
                pool.wait_ge(z_done, i * 4 + (k + 1))
                half = slice((k % 2) * HALF, (k % 2 + 1) * HALF)
                m = (k // 2) % 2
                nc.gpsimd.tensor_tensor(z[:, m, half], z[:, m, half], xc[:, m, half], ALU.add).then_inc(out_done, 1)

            for k in range(4):
                step(0, k)
            with pool.Fori(1, STEPS // 4 - 1) as i:
                for k in range(4):
                    step(i, k)
            for k in range(4):
                step(STEPS // 4 - 1, k)

        @block.scalar
        def _(act):
            act.wait_ge(in_small, 64)
            nc.scalar.activation(dt_c[:], ld[:], ACT.Exp).then_inc(dt_done, 1)
            nc.scalar.activation(small[:, 0, :], la[:], ACT.Exp).then_inc(dt_done, 1)
            act.wait_ge(red_half, 1)
            nc.scalar.activation(small[:, 5, :], small[:, 1, :], ACT.Tanh, scale=0.5).then_inc(sin_half, 1)
            nc.scalar.activation(small[:, 6:8, :], small[:, 3:5, :], ACT.Sin, scale=TURN).then_inc(sin_half, 1)
            act.wait_ge(mag_arg, 1)
            nc.scalar.activation(mag1[:], mag1[:], ACT.Exp).then_inc(mag_done, 1)
            act.wait_ge(mag_arg, 2)
            nc.scalar.activation(mag2[:], mag2[:], ACT.Exp).then_inc(mag_done, 1)
            for g in range(GROUPS):
                for n in range(3):
                    act.wait_ge(wave_arg, 3 * g + n + 1)
                    nc.scalar.activation(wave[:, n], wave[:, n], ACT.Sin, scale=-TURN,
                                         bias=phase[:, 3:4] if n == 2 else phase[:, 2:3]).then_inc(wave_done, 1)

            def split_x(i, m):
                act.wait_ge(xt_done, i * 2 + (m + 1))
                need(act, conv_done, i * 4 + (2 * m - 2))
                nc.scalar.copy(xh[:, m % 2, :, LAG0:, :],
                               ps_t[:].rearrange("p n f -> p (n f)").rearrange("p (j h b) -> p h j b", h=2, b=B)
                               ).then_inc(xh_done, 1)

            def split_w(i, k):
                act.wait_ge(w_loaded[k % 2], i * 32 + (16 * (k // 2) + 16))
                need(act, conv_done, i * 4 + (k - 1))
                nc.scalar.copy(wh[:, k % 2, :], wf[:, k % 2, :]).then_inc(wh_done, 1)

            split_x(0, 0)
            split_w(0, 0)

            def body1(i):
                for m in range(2):
                    split_w(i, 2 * m + 1)
                    if not isinstance(i, int) or 2 * i + m + 1 < PAIRS:
                        split_x(i, m + 1)
                        split_w(i, 2 * m + 2)

            body1(0)
            with act.Fori(1, C // 4 - 1) as i:
                body1(i)
            body1(C // 4 - 1)

            def split_sess(i, m):
                act.wait_ge(tables_done, 1)
                act.wait_ge(wg_loaded[m % 2], i * 32 + (32 * (m // 2) + 32))
                need(act, mm1_done, i * 4 + (2 * m - 2))
                q = i * 2 + m
                for b in range(2):
                    part = slice(b * C, (b + 1) * C)
                    nc.scalar.activation(wbh[part, m % 2, b, :], wg[part, m % 2, :], ACT.Copy,
                                         scale=cmask[part, bass.ds(q, 1)]).then_inc(wbh_done, 1)

            act.wait_ge(wb_zero, 4)

            def step(i, k):
                if isinstance(i, int) and 4 * i + k == -2:
                    split_sess(0, 0)
                if exists(i, k) and k % 2 == 0 and exists(i, k + 2):
                    split_sess(i, k // 2 + 1)
                if exists(i, k + 2):
                    act.wait_ge(xc_done, i * 4 + (k + 3))
                    need(act, mm1_done, i * 4 + (k + 1))
                    m = ((k + 2) // 2) % 2
                    half = slice((k % 2) * HALF, (k % 2 + 1) * HALF)
                    nc.scalar.copy(xch[:, k % 2, :], xc[:, m, half]).then_inc(xch_done, 1)
                if exists(i, k + 1):
                    n = (k + 1) % 2
                    act.wait_ge(tables_done, 1)
                    act.wait_ge(mm1_done, i * 4 + (k + 2))
                    need(act, mm2_done, i * 4 + k)
                    for b in range(2):
                        col = i * 4 + (2 * ((k + 1) // 2) + b)
                        nc.scalar.activation(hid[:, n, b, :], ps_h[:, n, b, :], ACT.Gelu,
                                             bias=bias_t[:, bass.ds(col, 1)]).then_inc(hid_done, 1)

            steps_of(act, step)

        @block.vector
        def _(dve):
            steps = [0]

            def link(ins):
                steps[0] += 1
                ins.then_inc(chain, 1)
                dve.wait_ge(chain, steps[0])

            nc.vector.memset(xh[:, :, :, 0:LAG0, :].bitcast(F32), 0.0).then_inc(x_zero, 1)
            nc.vector.memset(xl[:, :, :, 0:LAG0, :].bitcast(F32), 0.0).then_inc(x_zero, 1)
            for n, v in enumerate((0.25, 0.0)):
                part = slice(n * N, (n + 1) * N)
                nc.vector.memset(phase[part, 0:1], v)
                nc.vector.memset(phase[part, 1:2], v + 0.25)
                nc.vector.memset(phase[part, 2:3], v * TURN)
                last = nc.vector.memset(phase[part, 3:4], (v + 0.25) * TURN)
            link(last)

            s = [small[:, n, :] for n in range(20)]
            c_re, c_im = ccs[:, :, 0], ccs[:, :, 1]
            dve.wait_ge(dt_done, 2)
            TT, TS, STT = nc.vector.tensor_tensor, nc.vector.tensor_scalar, nc.vector.scalar_tensor_tensor
            TS(s[1], s[0], dt_c[:], -1.0, ALU.mult, ALU.mult)
            link(TS(s[2], ai[:], dt_c[:], INV_TURN, ALU.mult, ALU.mult))
            TS(s[8], s[2], 0.5, MAGIC, ALU.mult, ALU.add)
            link(TS(s[10], s[2], 0.5, 0.25, ALU.mult, ALU.add))
            TS(s[9], s[10], MAGIC, -MAGIC, ALU.add, ALU.add)
            link(TS(s[8], s[8], -MAGIC, None, ALU.add))
            STT(s[3], s[2], 0.5, s[8], ALU.mult, ALU.subtract)
            TT(s[4], s[10], s[9], ALU.subtract).then_inc(red_half, 1)
            TT(s[11], s[0], s[0], ALU.mult)
            link(TT(s[12], ai[:], ai[:], ALU.mult))
            link(TT(s[11], s[11], s[12], ALU.add))
            link(nc.vector.reciprocal(s[11], s[11]))
            dve.wait_ge(sin_half, 2)
            link(TS(s[12], s[5], -1.0, 1.0, ALU.mult, ALU.add))
            link(nc.vector.reciprocal(s[12], s[12]))
            STT(s[13], s[5], 2.0, s[12], ALU.mult, ALU.mult)
            STT(s[14], s[6], 2.0, s[6], ALU.mult, ALU.mult)
            link(STT(s[15], s[6], 2.0, s[7], ALU.mult, ALU.mult))
            TS(s[12], s[14], -1.0, 1.0, ALU.mult, ALU.add)
            link(STT(s[16], s[13], 1.0, s[15], ALU.add, ALU.mult))
            link(TT(s[12], s[13], s[12], ALU.mult))
            link(TT(s[12], s[12], s[14], ALU.subtract))
            TT(s[13], c_re, s[12], ALU.mult)
            TT(s[14], c_im, s[16], ALU.mult)
            TT(s[15], c_re, s[16], ALU.mult)
            link(TT(s[17], c_im, s[12], ALU.mult))
            TT(s[13], s[13], s[14], ALU.subtract)
            link(TT(s[15], s[15], s[17], ALU.add))
            TT(s[12], s[13], s[0], ALU.mult)
            TT(s[14], s[15], ai[:], ALU.mult)
            TT(s[16], s[13], ai[:], ALU.mult)
            link(TT(s[17], s[15], s[0], ALU.mult))
            TT(s[14], s[14], s[12], ALU.subtract)
            link(TT(s[16], s[16], s[17], ALU.add))
            for n in range(2):
                part = slice(n * N, (n + 1) * N)
                sign = 1.0 - 2.0 * n
                nc.vector.tensor_copy(stack[:, 0, part], s[2])
                nc.vector.tensor_copy(stack[:, 1, part], s[1])
                STT(stack[:, 2, part], s[14], 2.0 * sign, s[11], ALU.mult, ALU.mult)
                STT(stack[:, 3, part], s[16], -2.0 * sign, s[11], ALU.mult, ALU.mult).then_inc(stack_done, 1)

            dve.wait_ge(iota_done, 7)
            link(nc.vector.tensor_copy(exps[:], exps_i[:]))
            dve.wait_ge(par_t, 1)
            link(nc.vector.tensor_copy(par[:], ps_h[:, 1, 0, 0:4 * C].rearrange("p (q h) -> p q h", q=4)))

            def spread(q, hs):
                return par[:, q, hs].unsqueeze(2).to_broadcast([P, hs.stop - hs.start, RAD])

            def expo(n, count):
                return exps[:, n, :].unsqueeze(1).to_broadcast([P, count, RAD])

            every = slice(0, C)
            TT(mag1[:], spread(1, every), expo(0, C), ALU.mult).then_inc(mag_arg, 1)
            TT(mag2[:], spread(1, every), expo(1, C), ALU.mult).then_inc(mag_arg, 1)
            for g in range(GROUPS):
                hs = slice(GC * g, GC * (g + 1))
                TT(turns[:, 0], spread(0, hs), expo(0, GC), ALU.mult)
                link(TT(turns[:, 1], spread(0, hs), expo(1, GC), ALU.mult))
                for n, (t, ph) in enumerate(((0, 0), (1, 0), (1, 1))):
                    last = TS(nearest[:, n], turns[:, t], phase[:, ph:ph + 1], MAGIC, ALU.add, ALU.add)
                link(last)
                for n, t in enumerate((0, 1, 1)):
                    STT(wave[:, n], nearest[:, n], MAGIC, turns[:, t], ALU.subtract, ALU.subtract
                        ).then_inc(wave_arg, 1)
                if g == 0:
                    dve.wait_ge(mag_done, 2)
                if g >= 2:
                    dve.wait_ge(k_done, g - 1)
                dve.wait_ge(wave_done, 3 * g + 1)
                TT(e1[:, g % 2], wave[:, 0], mag1[:, hs], ALU.mult)
                dve.wait_ge(wave_done, 3 * g + 3)
                TT(wave[:, 1], wave[:, 1], spread(2, hs), ALU.mult)
                link(TT(wave[:, 2], wave[:, 2], spread(3, hs), ALU.mult))
                link(TT(wave[:, 1], wave[:, 1], wave[:, 2], ALU.add))
                TT(e2[:, g % 2], wave[:, 1], mag2[:, hs], ALU.mult).then_inc(e_done, 1)
                if g == 0:
                    dve.wait_ge(in_ints, 64)
                    nc.vector.tensor_copy(time_rev[:], time_i[:])
                    nc.vector.tensor_copy(row_t[:], row_i[:])
                    nc.vector.tensor_copy(chan_of[:], chan_i[:])
                    nc.vector.tensor_copy(sess_of[:], sess_i[:])
                    link(nc.vector.tensor_copy(ints_f[:], ints[:]))
                    TT(mask1[:], time_rev[:].unsqueeze(2).to_broadcast([P, CH, B]),
                       ints_f[:, 0, :].unsqueeze(1).to_broadcast([P, CH, B]), ALU.is_lt)
                    TS(onehot[:], ints_f[0:SESS, 3, :], sess_of[:], None, ALU.is_equal).then_inc(onehot_done, 1)
                    for n in range(2):
                        part = slice(n * C, (n + 1) * C)
                        own = ints_f[part].rearrange("p v (q b) -> p v q b", b=2)
                        nc.vector.tensor_copy(len2_p[part, :], own[:, 1, :, n])
                        last = TS(cmask[part, :], own[:, 2, :, n], chan_of[part, :], None, ALU.is_gt)
                    link(last)
                    dve.wait_ge(in_d, 64)
                if g >= 1:
                    finish_kernel = g - 1
                    dve.wait_ge(k_done, g)
                    TT(krow[:, finish_kernel], ps_h[:, 0, (g - 1) % 2, 0:P].rearrange("p (h b) -> p h b", b=RAD),
                       dplace[:, GC // QUAD * (g - 1):GC // QUAD * g, :], ALU.add).then_inc(krow_done, 1)
            g = GROUPS
            dve.wait_ge(k_done, g)
            TT(krow[:, g - 1], ps_h[:, 0, (g - 1) % 2, 0:P].rearrange("p (h b) -> p h b", b=RAD),
               dplace[:, GC // QUAD * (g - 1):GC // QUAD * g, :], ALU.add).then_inc(krow_done, 1)
            dve.wait_ge(bias_mm, 1)
            nc.vector.tensor_copy(bias_t[:], ps_h[:, 1, 1, 0:B]).then_inc(tables_done, 1)

            def split_x(i, m):
                dve.wait_ge(xh_done, i * 2 + (m + 1))
                nc.vector.tensor_tensor(
                    xl[:, m % 2, :, LAG0:, :],
                    ps_t[:].rearrange("p n f -> p (n f)").rearrange("p (j h b) -> p h j b", h=2, b=B),
                    xh[:, m % 2, :, LAG0:, :], ALU.subtract).then_inc(xl_done, 1)

            def split_w(i, k):
                dve.wait_ge(wh_done, i * 4 + (k + 1))
                nc.vector.tensor_tensor(wl[:, k % 2, :], wf[:, k % 2, :], wh[:, k % 2, :],
                                        ALU.subtract).then_inc(wl_done, 1)

            def keep_y(i, k):
                dve.wait_ge(conv_done, i * 4 + (k + 1))
                nc.vector.tensor_tensor(
                    y[:, :, :, :, bass.ds(i * 4 + k, 1)].rearrange("p q i b c -> p i q (b c)"),
                    ps_y[:, k % 2, :].rearrange("p (i q b) -> p i q b", i=CH, b=2),
                    mask1[:].rearrange("p i (q b) -> p i q b", b=2), ALU.mult).then_inc(y_done, 1)

            for g in range(GROUPS):
                dve.wait_ge(k_stored[g], 16 * QUAD)
            dve.wait_ge(k_pad, 16)
            split_x(0, 0)
            split_w(0, 0)

            def body1(i):
                for m in range(2):
                    split_w(i, 2 * m + 1)
                    keep_y(i, 2 * m)
                    if not isinstance(i, int) or 2 * i + m + 1 < PAIRS:
                        split_x(i, m + 1)
                        split_w(i, 2 * m + 2)
                    keep_y(i, 2 * m + 1)

            body1(0)
            with dve.Fori(1, C // 4 - 1) as i:
                body1(i)
            body1(C // 4 - 1)

            for t in (wbh, wbl):
                for b in range(2):
                    nc.vector.memset(t[(1 - b) * C:(2 - b) * C, :, b, :].bitcast(F32), 0.0).then_inc(wb_zero, 1)

            def split_sess(i, m):
                dve.wait_ge(wbh_done, i * 4 + (2 * m + 2))
                q = i * 2 + m
                for b in range(2):
                    part = slice(b * C, (b + 1) * C)
                    last = nc.vector.scalar_tensor_tensor(
                        wbl[part, m % 2, b, :], wg[part, m % 2, :], cmask[part, bass.ds(q, 1)],
                        wbh[part, m % 2, b, :], ALU.mult, ALU.subtract)
                last.then_inc(wbl_done, 1)

            def step(i, k):
                hf = k % 2
                half = slice(hf * HALF, (hf + 1) * HALF)
                if exists(i, k + 2):
                    m = ((k + 2) // 2) % 2
                    dve.wait_ge(t2_done, i * 4 + (k + 3))
                    if k % 2 == 0:
                        dve.wait_ge(xn_loaded[m], i * 16 + (16 * ((k + 2) // 4) + 16))
                    need(dve, out_done, i * 4 + (k - 1))
                    nc.vector.tensor_tensor(
                        xc[:, m, half].rearrange("p (i t) -> p i t", t=P),
                        ps_t[:, hf, :].rearrange("p (i t) -> p i t", t=P)[:, :, ::-1],
                        xin[:, m, half].rearrange("p (i t) -> p i t", t=P), ALU.add).then_inc(xc_done, 1)
                if isinstance(i, int) and 4 * i + k == -2:
                    split_sess(0, 0)
                if exists(i, k) and k % 2 == 0 and exists(i, k + 2):
                    split_sess(i, k // 2 + 1)
                if exists(i, k):
                    need(dve, z_done, i * 4 + (k - 1))
                    q = i * 2 + k // 2
                    nc.vector.tensor_scalar(tmask[:, hf, :], row_t[:, half], len2_p[:, bass.ds(q, 1)], None,
                                            ALU.is_lt).then_inc(tmask_done, 1)
                if exists(i, k + 2):
                    m = ((k + 2) // 2) % 2
                    dve.wait_ge(xch_done, i * 4 + (k + 3))
                    nc.vector.tensor_tensor(xcl[:, hf, :], xc[:, m, half], xch[:, hf, :],
                                            ALU.subtract).then_inc(xcl_done, 1)
                if exists(i, k):
                    m = (k // 2) % 2
                    dve.wait_ge(mm2_done, i * 4 + (k + 1))
                    dve.wait_ge(tmask_done, i * 4 + (k + 1))
                    if hf == 0:
                        need(dve, stored[m], i * 16 + 0)
                    nc.vector.scalar_tensor_tensor(z[:, m, half], ps_y[:, hf, :], b2_col[:], tmask[:, hf, :],
                                                   ALU.add, ALU.mult).then_inc(z_done, 1)

            dve.wait_ge(in_late, 64)
            steps_of(dve, step)

        @block.tensor
        def _(pe):
            def transpose_x(i, m):
                pe.wait_ge(x_loaded[m % 2], i * 32 + (32 * (m // 2) + 32))
                need(pe, xl_done, i * 2 + m)
                for j in range(CH):
                    last = nc.tensor.transpose(ps_t[:, j // 4, (j % 4) * P:(j % 4 + 1) * P],
                                               xin[:, m % 2, j * P:(j + 1) * P], ident[:])
                last.then_inc(xt_done, 1)

            pe.wait_ge(ident_done, 2)
            transpose_x(0, 0)
            pe.wait_ge(stack_done, 2)
            for q in range(4):
                last = nc.tensor.transpose(ps_h[:, 1, 0, q * C:(q + 1) * C], stack[:, q, :], ident[0:C, 0:C])
            last.then_inc(par_t, 1)
            for g in range(GROUPS):
                pe.wait_ge(e_done, g + 1)
                if g >= 2:
                    pe.wait_ge(krow_done, g - 1)
                for h in range(GC):
                    q, col = h % QUAD, h // QUAD
                    last = nc.tensor.matmul(ps_h[RAD * q:RAD * (q + 1), 0, g % 2, col * RAD:(col + 1) * RAD],
                                            e2[:, g % 2, h, :], e1[:, g % 2, h, :], start=True, stop=True)
                last.then_inc(k_done, 1)
            pe.wait_ge(onehot_done, 1)
            pe.wait_ge(in_late, 64)
            nc.tensor.matmul(ps_h[:, 1, 1, 0:B], bs[:], onehot[:], start=True, stop=True).then_inc(bias_mm, 1)

            def conv(i, k):
                n, h, xs = k % 2, k % 2, (k // 2) % 2
                pe.wait_ge(wl_done, i * 4 + (k + 1))
                pe.wait_ge(xl_done, i * 2 + (k // 2 + 1))
                need(pe, y_done, i * 4 + (k - 1))
                for d in range(CH):
                    first = min(d, CH - 4)
                    src = slice(LAG0 + first - d, LAG0 + CH - d)
                    cols = slice(T - P * (d + 1), T - P * d)
                    for t, (w, v) in enumerate(((wh, xh), (wh, xl), (wl, xh))):
                        last = nc.tensor.matmul(ps_y[:, n, first * B:], w[:, n, cols], v[:, xs, h, src, :],
                                                start=(d == 0 and t == 0), stop=(d == CH - 1 and t == 2))
                last.then_inc(conv_done, 1)

            pe.wait_ge(x_zero, 2)

            def body1(i):
                for m in range(2):
                    conv(i, 2 * m)
                    if not isinstance(i, int) or 2 * i + m + 1 < PAIRS:
                        transpose_x(i, m + 1)
                    conv(i, 2 * m + 1)

            body1(0)
            with pe.Fori(1, C // 4 - 1) as i:
                body1(i)
            body1(C // 4 - 1)

            pe.wait_ge(xl_done, PAIRS)
            pe.wait_ge(y_done, C)

            def step(i, k):
                if exists(i, k + 2):
                    hf, m = k % 2, ((k + 2) // 2) % 2
                    if hf == 0:
                        pe.wait_ge(ys_loaded[m], i * 16 + (16 * ((k + 2) // 4) + 16))
                    need(pe, xc_done, i * 4 + (k + 1))
                    for j in range(4):
                        last = nc.tensor.transpose(ps_t[:, hf, j * P:(j + 1) * P], ys[:, m, 4 * hf + j, :], ident[:])
                    last.then_inc(t2_done, 1)
                if exists(i, k + 1):
                    hf, m = (k + 1) % 2, ((k + 1) // 2) % 2
                    pe.wait_ge(xcl_done, i * 4 + (k + 2))
                    pe.wait_ge(wbl_done, i * 2 + ((k + 1) // 2 + 1))
                    need(pe, hid_done, i * 8 + 2 * k)
                    for b in range(2):
                        for t, (w, v) in enumerate(((wbh, xch), (wbh, xcl), (wbl, xch))):
                            last = nc.tensor.matmul(ps_h[:, hf, b, :], w[:, m, b, :], v[:, hf, :],
                                                    start=(t == 0), stop=(t == 2))
                    last.then_inc(mm1_done, 1)
                if exists(i, k):
                    hf = k % 2
                    pe.wait_ge(hid_done, i * 8 + (2 * k + 2))
                    need(pe, z_done, i * 4 + (k - 1))
                    for b in range(2):
                        last = nc.tensor.matmul(ps_y[b * C:(b + 1) * C, hf, :], w2_s[:], hid[:, hf, b, :],
                                                start=True, stop=True)
                    last.then_inc(mm2_done, 1)

            steps_of(pe, step)


_INS = ["x", "itok_B_78_3631", "itok_B_0_7", "itok_B_2182_4065", "_lenS", "L0_cond_log_dt", "L0_cond_C",
        "L0_cond_log_A_real", "L0_cond_A_imag", "L0_cond_D", "L1_cond_W_sess", "L1_cond_b_sess", "L1_cond_W2",
        "L1_cond_b2"]


def kernel(**inputs):
    import numpy as np
    import concourse.bacc as bacc
    from concourse.bass_utils import run_bass_kernel_spmd

    nc = bacc.Bacc("TRN2", target_bir_lowering=False, num_devices=1)
    arrays, args = {}, []
    for name in _INS:
        a = np.ascontiguousarray(inputs[name])
        arrays[f"in_{name}"] = a
        args.append(nc.dram_tensor(f"in_{name}", a.shape, mybir.dt.from_np(a.dtype), kind="ExternalInput").ap())
    args.append(nc.dram_tensor("out_0", (B, C, T), F32, kind="ExternalOutput").ap())
    x, len1, sid, len2, chans, log_dt, cc, log_a, a_imag, dskip, w_sess, b_sess, w2, b2, out = args
    build_program(nc, x, len1, sid, len2, chans, log_dt, cc, log_a, a_imag, dskip, w_sess, b_sess, w2, b2, out)
    r = run_bass_kernel_spmd(nc, [arrays], core_ids=[0])
    return r.results[0]["out_0"]
```

```python
import math
from contextlib import ExitStack

import concourse.bass as bass
from concourse import mybir

F32 = mybir.dt.float32
F32R = mybir.dt.float32r
I32 = mybir.dt.int32
F16 = mybir.dt.float16
ALU = mybir.AluOpType
ACT = mybir.ActivationFunctionType

B, C, T = 64, 64, 1024
N = 64
HID, SESS = 128, 8
P = 128
CH = T // P
PAIRS = C // 2
HALF = T // 2
RAD = 32
FAR = 5
NEAR0 = T - P * FAR
WSLOTS = 4
KPAD = T + P
QUAD = 4
BODIES = C // QUAD
AHEAD = 2
MAGIC = 1.5 * 2.0 ** 23
TURN = 6.283185
INV_TURN = 1.0 / (2.0 * math.pi)
LN2_HI = 0.693359375
LN2_LO = math.log(2.0) - LN2_HI


def need(eng, sem, value):
    if isinstance(value, int) and value <= 0:
        return
    eng.wait_ge(sem, value)


def build_program(nc, x, len1, sid, len2, chans, log_dt, cc, log_a, a_imag, dskip, w_sess, b_sess, w2, b2, out):
    kr = nc.dram_tensor("kr", (C, KPAD), F32, kind="Internal").ap()
    x_rows = x.rearrange("b c t -> (b c) t")
    out_rows = out.rearrange("b c t -> (b c) t")
    toeplitz = bass.AP(kr.tensor, 0, [[KPAD, C], [1, P], [1, T]])

    ctx = ExitStack()
    early = ExitStack()
    late = ExitStack()
    with ctx:
        def sb(name, shape, dt=F32, where=ctx):
            return where.enter_context(nc.sbuf_tensor(name, shape, dt))

        def sem(name):
            return ctx.enter_context(nc.semaphore(name))

        ident = sb("ident", [P, P])
        mask1 = sb("mask1", [P, CH, B])
        row_t = sb("row_t", [P, T], F16)
        sids = sb("sids", [1, B], I32)
        len2_p = sb("len2_p", [P, PAIRS])
        cmask = sb("cmask", [P, PAIRS])
        bias_t = sb("bias_t", [P, B])
        w2_s = sb("w2_s", [HID, C])
        b2_col = sb("b2_col", [P, 1])

        xin = sb("xin", [P, 2, T])
        ones = sb("ones", [P, P], where=early)
        row_i = sb("row_i", [P, T], I32, where=early)
        time_i = sb("time_i", [P, CH], I32, where=early)
        time_rev = sb("time_rev", [P, CH], where=early)
        chan_i = sb("chan_i", [P, 1], I32, where=early)
        chan_of = sb("chan_of", [P, 1], where=early)
        ints = sb("ints", [P, 4, B], I32, where=early)
        ints_f = sb("ints_f", [P, 4, B], where=early)
        sess_i = sb("sess_i", [SESS, 1], I32, where=early)
        sess_of = sb("sess_of", [SESS, 1], where=early)
        onehot = sb("onehot", [SESS, B], where=early)
        bs = sb("bs", [SESS, HID], where=early)
        la = sb("la", [C, N], where=early)
        ai = sb("ai", [C, N], where=early)
        ccs = sb("ccs", [C, N, 2], where=early)
        ld = sb("ld", [C, 1], where=early)
        power = sb("power", [C, 1], I32, where=early)
        tiny = sb("tiny", [C, 4], where=early)
        dt_c = sb("dt_c", [C, 1], where=early)
        small = sb("small", [C, 18, N], where=early)
        stack = sb("stack", [C, 4, P], where=early)
        exps_i = sb("exps_i", [P, 2, RAD], I32, where=early)
        zrow = sb("zrow", [C, P], where=early)
        early.close()
        y = sb("y", [P, PAIRS, CH, 2, C])
        par = sb("par", [P, 4, C], where=late)
        exps = sb("exps", [P, 2, RAD], where=late)
        phase = sb("phase", [P, 4], where=late)
        mag = sb("mag", [P, 2, C, RAD], where=late)
        turns = sb("turns", [P, 2, QUAD, RAD], where=late)
        nearest = sb("nearest", [P, 3, QUAD, RAD], where=late)
        wave = sb("wave", [P, 3, QUAD, RAD], where=late)
        e1 = sb("e1", [P, QUAD, RAD], where=late)
        e2 = sb("e2", [P, QUAD, RAD], where=late)
        dplace = sb("dplace", [P, BODIES, RAD], where=late)
        krow = sb("krow", [P, RAD], where=late)
        wf = sb("wf", [P, WSLOTS, T], where=late)
        wh = sb("wh", [P, 2, T - NEAR0], F32R, where=late)
        wl = sb("wl", [P, 2, T - NEAR0], F32R, where=late)
        xh = sb("xh", [P, 2, 2, CH, B], F32R, where=late)
        xl = sb("xl", [P, 2, 2, CH, B], F32R, where=late)
        xf = sb("xf", [P, 2, 2, 1 + CH - FAR, B], where=late)
        late.close()
        ys = sb("ys", [P, 2, CH, P])
        xc = sb("xc", [P, 2, T])
        xch = sb("xch", [P, 2, HALF], F32R)
        xcl = sb("xcl", [P, 2, HALF], F32R)
        hid = sb("hid", [P, 2, 2, HALF])
        tmask = sb("tmask", [P, 2, HALF], F16)
        z = sb("z", [P, 2, T])
        wg = sb("wg", [P, 2, HID])
        wbh = sb("wbh", [P, 2, 2, HID], F32R)
        wbl = sb("wbl", [P, 2, 2, HID], F32R)

        ps_t = ctx.enter_context(nc.psum_tensor("ps_t", [P, 2, 512], F32))
        ps_y = ctx.enter_context(nc.psum_tensor("ps_y", [P, 2, 512], F32))
        ps_h = ctx.enter_context(nc.psum_tensor("ps_h", [P, 2, 2, 512], F32))

        in_ld = sem("in_ld")
        in_la = sem("in_la")
        in_ai = sem("in_ai")
        in_ints = sem("in_ints")
        in_sids = sem("in_sids")
        in_late = sem("in_late")
        in_d = sem("in_d")
        ident_done = sem("ident_done")
        iota_done = sem("iota_done")
        d_zero = sem("d_zero")
        chain = sem("chain")
        abs_done = sem("abs_done")
        red_half = sem("red_half")
        sin_half = sem("sin_half")
        stack_done = sem("stack_done")
        par_t = sem("par_t")
        par_done = sem("par_done")
        mag_arg = sem("mag_arg")
        mag_rest = sem("mag_rest")
        mag_done = sem("mag_done")
        maker = sem("maker")
        wave_arg = sem("wave_arg")
        wave_done = sem("wave_done")
        sum_done = sem("sum_done")
        e_done = sem("e_done")
        k_done = sem("k_done")
        krow_done = sem("krow_done")
        k_pad = sem("k_pad")
        k_stored = sem("k_stored")
        onehot_done = sem("onehot_done")
        bias_mm = sem("bias_mm")
        tables_done = sem("tables_done")
        x_zero = sem("x_zero")
        x_loaded = [sem(f"x_loaded{n}") for n in range(2)]
        w_loaded = [sem(f"w_loaded{n}") for n in range(WSLOTS)]
        xt_done = sem("xt_done")
        xh_done = sem("xh_done")
        xl_done = sem("xl_done")
        wh_done = sem("wh_done")
        wl_done = sem("wl_done")
        conv_done = sem("conv_done")
        y_done = sem("y_done")
        xn_loaded = [sem(f"xn_loaded{n}") for n in range(2)]
        ys_loaded = [sem(f"ys_loaded{n}") for n in range(2)]
        wg_loaded = [sem(f"wg_loaded{n}") for n in range(2)]
        wb_zero = sem("wb_zero")
        wbh_done = sem("wbh_done")
        wbl_done = sem("wbl_done")
        t2_done = sem("t2_done")
        xc_done = sem("xc_done")
        xch_done = sem("xch_done")
        xcl_done = sem("xcl_done")
        mm1_done = sem("mm1_done")
        hid_done = sem("hid_done")
        mm2_done = sem("mm2_done")
        tmask_done = sem("tmask_done")
        z_done = sem("z_done")
        out_done = sem("out_done")
        stored = [sem(f"stored{n}") for n in range(2)]

        block = ctx.enter_context(nc.Block())

        STEPS = 2 * PAIRS

        def steps_of(eng, step):
            for k in (2, 3):
                step(-1, k)
            for k in range(4):
                step(0, k)
            with eng.Fori(1, STEPS // 4 - 1) as i:
                for k in range(4):
                    step(i, k)
            for k in range(4):
                step(STEPS // 4 - 1, k)

        def rounds_of(eng, body):
            body(0)
            with eng.Fori(1, BODIES - AHEAD) as i:
                body(i)
            for i in range(BODIES - AHEAD, BODIES):
                body(i)

        def makes(i):
            return not isinstance(i, int) or i < BODIES - AHEAD

        def exists(i, k):
            return not isinstance(i, int) or 0 <= 4 * i + k < STEPS

        @block.sync
        def _(sp):
            sp.dma_start(ld[:], log_dt.rearrange("(h a) -> h a", a=1)).then_inc(in_ld, 16)
            sp.dma_start(la[:], log_a).then_inc(in_la, 16)

            def load_x(i, m):
                need(sp, xt_done, i * 2 + (m - 1))
                for h in range(2):
                    src = x[:, bass.ds(i * 4 + (2 * m + h), 1), :].rearrange("b c t -> (b c) t")
                    sp.dma_start(xin[h * B:(h + 1) * B, m % 2, :], src).then_inc(x_loaded[m % 2], 16)

            def load_w(i, k):
                need(sp, conv_done, i * 4 + (k - WSLOTS + 1))
                src = toeplitz[bass.ds(i * 4 + k, 1)].rearrange("h s c -> (h s) c")
                sp.dma_start(wf[:, k % WSLOTS, :], src).then_inc(w_loaded[k % WSLOTS], 16)

            def store_kernels(j):
                sp.wait_ge(krow_done, j + 1)
                dst = kr[bass.ds(j * QUAD, QUAD), 0:T].rearrange("h (a b) -> h a b", b=RAD)
                for q in range(QUAD):
                    sp.dma_start(dst[q], krow[RAD * q:RAD * (q + 1), :]).then_inc(k_stored, 16)

            load_x(0, 0)
            for n, v in enumerate((len1, len2, chans, sid)):
                sp.dma_start(ints[:, n, :], bass.AP(v.tensor, 0, [[0, P], [1, B]])).then_inc(in_ints, 16)
            sp.dma_start(sids[:], sid.rearrange("(a b) -> a b", a=1)).then_inc(in_sids, 16)
            load_x(0, 1)
            sp.wait_ge(d_zero, 1)
            for q in range(QUAD):
                sp.dma_start(dplace[RAD * q + RAD - 1:RAD * q + RAD, :, RAD - 1:RAD],
                             bass.AP(dskip.tensor, q, [[C, 1], [QUAD, BODIES], [1, 1]]),
                             allow_slow_non_contiguous=True).then_inc(in_d, 16)
            sp.dma_start(kr[:, T:KPAD], zrow[:]).then_inc(k_pad, 16)
            sp.dma_start(bs[:], b_sess).then_inc(in_late, 16)
            sp.dma_start(w2_s[:], w2).then_inc(in_late, 16)
            for n in range(2):
                sp.dma_start(b2_col[n * C:(n + 1) * C, :], b2.rearrange("(s a) -> s a", a=1)).then_inc(in_late, 16)
            load_x(0, 2)
            sp.wait_ge(k_pad, 16)

            store_kernels(0)
            sp.wait_ge(k_stored, 16 * QUAD)
            for k in range(WSLOTS):
                load_w(0, k)
            store_kernels(1)

            def body1(i):
                if makes(i) or i < BODIES - 1:
                    sp.wait_ge(k_stored, i * (16 * QUAD) + 2 * 16 * QUAD)
                    load_x(i, 3)
                    load_w(i, 4)
                    load_w(i, 5)
                if makes(i):
                    load_x(i, 4)
                    store_kernels(i + AHEAD)
                if makes(i) or i < BODIES - 1:
                    load_w(i, 6)
                    load_w(i, 7)

            rounds_of(sp, body1)

            def load_pair(i, m):
                need(sp, t2_done, i * 4 + (2 * m - 2))
                q = i * 2 + m
                sp.dma_start(ys[:, m % 2, :, :].rearrange("p i n -> p (i n)"),
                             y[:, bass.ds(q, 1), :, :, :].rearrange("p q i b c -> p (q i b c)")
                             ).then_inc(ys_loaded[m % 2], 16)
                need(sp, xc_done, i * 4 + (2 * m - 2))
                sp.dma_start(xin[:, m % 2, :], x_rows[bass.ds(i * (2 * P) + m * P, P), :]
                             ).then_inc(xn_loaded[m % 2], 16)
                need(sp, wbl_done, i * 2 + (m - 1))
                for b in range(2):
                    s = sp.value_load(sids[0:1, bass.ds(i * 4 + (2 * m + b), 1)], min_val=0, max_val=SESS - 1)
                    sp.dma_start(wg[b * C:(b + 1) * C, m % 2, :],
                                 w_sess[bass.ds(s, 1)].rearrange("s c n -> (s c) n")).then_inc(wg_loaded[m % 2], 16)

            def store_pair(i, m):
                sp.wait_ge(out_done, i * 4 + (2 * m + 2))
                sp.dma_start(out_rows[bass.ds(i * (2 * P) + m * P, P), :], z[:, m % 2, :]
                             ).then_inc(stored[m % 2], 16)

            sp.wait_ge(xt_done, PAIRS)
            sp.wait_ge(y_done, C)
            sp.wait_ge(in_sids, 16)
            load_pair(0, 0)
            load_pair(0, 1)

            def moves2(i):
                for m in range(2):
                    if not isinstance(i, int) or 2 * i + m + 2 < PAIRS:
                        load_pair(i, m + 2)
                    if not isinstance(i, int) or 2 * i + m > 0:
                        store_pair(i - (1 - m), 1 - m)

            moves2(0)
            with sp.Fori(1, PAIRS // 2 - 1) as i:
                moves2(i)
            moves2(PAIRS // 2 - 1)
            store_pair(PAIRS // 2 - 1, 1)
            for n in range(2):
                sp.wait_ge(stored[n], 16 * (PAIRS // 2))

        @block.gpsimd
        def _(pool):
            nc.gpsimd.memset(dplace[:], 0.0)
            nc.gpsimd.memset(zrow[:], 0.0).then_inc(d_zero, 1)
            nc.gpsimd.memset(ones[:], 1.0).then_inc(ident_done, 1)
            pool.wait_ge(ident_done, 1)
            nc.gpsimd.affine_select(out=ident[:], in_=ones[:], compare_op=ALU.is_equal, fill=0.0, base=0,
                                    pattern=[[-1, P]], channel_multiplier=1).then_inc(ident_done, 1)
            nc.gpsimd.iota(exps_i[:, 0, :], pattern=[[-1, RAD]], base=RAD - 1, channel_multiplier=0).then_inc(iota_done, 1)
            nc.gpsimd.iota(exps_i[:, 1, :], pattern=[[-RAD, RAD]], base=RAD * (RAD - 1),
                           channel_multiplier=0).then_inc(iota_done, 1)
            nc.gpsimd.iota(time_i[:], pattern=[[P, CH]], base=P - 1, channel_multiplier=-1).then_inc(iota_done, 1)
            nc.gpsimd.iota(row_i[:], pattern=[[1, T]], base=0, channel_multiplier=0).then_inc(iota_done, 1)
            for n in range(2):
                pool.wait_ge(iota_done, 4 + n)
                nc.gpsimd.iota(chan_i[n * C:(n + 1) * C, :], pattern=[[0, 1]], base=0,
                               channel_multiplier=1).then_inc(iota_done, 1)
            pool.wait_ge(iota_done, 6)
            nc.gpsimd.iota(sess_i[:], pattern=[[0, 1]], base=0, channel_multiplier=1).then_inc(iota_done, 1)

            pool.wait_ge(par_done, 1)
            rest = slice(AHEAD * QUAD, C)
            count = C - AHEAD * QUAD
            nc.gpsimd.tensor_tensor(
                mag[:, :, rest, :], par[:, 1, rest].unsqueeze(1).unsqueeze(3).to_broadcast([P, 2, count, RAD]),
                exps[:].unsqueeze(2).to_broadcast([P, 2, count, RAD]), ALU.mult).then_inc(mag_rest, 1)

            def step(i, k):
                if not exists(i, k):
                    return
                pool.wait_ge(z_done, i * 4 + (k + 1))
                half = slice((k % 2) * HALF, (k % 2 + 1) * HALF)
                m = (k // 2) % 2
                nc.gpsimd.tensor_tensor(z[:, m, half], z[:, m, half], xc[:, m, half], ALU.add).then_inc(out_done, 1)

            for k in range(4):
                step(0, k)
            with pool.Fori(1, STEPS // 4 - 1) as i:
                for k in range(4):
                    step(i, k)
            for k in range(4):
                step(STEPS // 4 - 1, k)

        @block.scalar
        def _(act):
            act.dma_start(ai[:], a_imag).then_inc(in_ai, 16)
            act.dma_start(ccs[:], cc).then_inc(in_ai, 16)
            act.wait_ge(in_la, 16)
            nc.scalar.activation(small[:, 0, :], la[:], ACT.Exp).then_inc(abs_done, 1)
            act.wait_ge(red_half, 1)
            nc.scalar.activation(small[:, 5, :], small[:, 1, :], ACT.Tanh, scale=0.5).then_inc(sin_half, 1)
            nc.scalar.activation(small[:, 6:8, :], small[:, 3:5, :], ACT.Sin, scale=TURN).then_inc(sin_half, 1)
            first = slice(0, AHEAD * QUAD)
            act.wait_ge(mag_arg, 1)
            nc.scalar.activation(mag[:, :, first, :], mag[:, :, first, :], ACT.Exp).then_inc(mag_done, 1)

            def waves(j):
                act.wait_ge(wave_arg, j * 2 + 1)
                nc.scalar.activation(wave[:, 0:2], wave[:, 0:2], ACT.Sin, scale=-TURN, bias=phase[:, 2:3]
                                     ).then_inc(wave_done, 1)
                act.wait_ge(wave_arg, j * 2 + 2)
                nc.scalar.activation(wave[:, 2], wave[:, 2], ACT.Sin, scale=-TURN, bias=phase[:, 3:4]
                                     ).then_inc(wave_done, 1)

            waves(0)
            waves(1)
            rest = slice(AHEAD * QUAD, C)
            act.wait_ge(mag_rest, 1)
            nc.scalar.activation(mag[:, :, rest, :], mag[:, :, rest, :], ACT.Exp).then_inc(mag_done, 1)

            def split_x(i, m):
                act.wait_ge(xt_done, i * 2 + (m + 1))
                need(act, conv_done, i * 4 + (2 * m - 2))
                xt = ps_t[:].rearrange("p n f -> p (n f)").rearrange("p (j h b) -> p h j b", h=2, b=B)
                nc.scalar.copy(xf[:, m % 2, :, 1:, :], xt[:, :, 0:CH - FAR, :])
                nc.scalar.copy(xh[:, m % 2], xt).then_inc(xh_done, 1)

            def split_w(i, k):
                act.wait_ge(w_loaded[k % WSLOTS], i * 16 + (16 * (k // WSLOTS) + 16))
                need(act, conv_done, i * 4 + (k - 1))
                nc.scalar.copy(wh[:, k % 2, :], wf[:, k % WSLOTS, NEAR0:]).then_inc(wh_done, 1)

            split_x(0, 0)
            split_w(0, 0)

            def body1(i):
                for m in range(2):
                    split_w(i, 2 * m + 1)
                    if makes(i) or 2 * i + m + 1 < PAIRS:
                        split_x(i, m + 1)
                        if m == 0 and makes(i):
                            waves(i + AHEAD)
                        split_w(i, 2 * m + 2)

            rounds_of(act, body1)

            def split_sess(i, m):
                act.wait_ge(tables_done, 1)
                act.wait_ge(wg_loaded[m % 2], i * 32 + (32 * (m // 2) + 32))
                need(act, mm1_done, i * 4 + (2 * m - 2))
                q = i * 2 + m
                for b in range(2):
                    part = slice(b * C, (b + 1) * C)
                    nc.scalar.activation(wbh[part, m % 2, b, :], wg[part, m % 2, :], ACT.Copy,
                                         scale=cmask[part, bass.ds(q, 1)]).then_inc(wbh_done, 1)

            act.wait_ge(wb_zero, 4)

            def step(i, k):
                if isinstance(i, int) and 4 * i + k == -2:
                    split_sess(0, 0)
                if exists(i, k) and k % 2 == 0 and exists(i, k + 2):
                    split_sess(i, k // 2 + 1)
                if exists(i, k + 2):
                    act.wait_ge(xc_done, i * 4 + (k + 3))
                    need(act, mm1_done, i * 4 + (k + 1))
                    m = ((k + 2) // 2) % 2
                    half = slice((k % 2) * HALF, (k % 2 + 1) * HALF)
                    nc.scalar.copy(xch[:, k % 2, :], xc[:, m, half]).then_inc(xch_done, 1)
                if exists(i, k + 1):
                    n = (k + 1) % 2
                    act.wait_ge(tables_done, 1)
                    act.wait_ge(mm1_done, i * 4 + (k + 2))
                    need(act, mm2_done, i * 4 + k)
                    for b in range(2):
                        col = i * 4 + (2 * ((k + 1) // 2) + b)
                        nc.scalar.activation(hid[:, n, b, :], ps_h[:, n, b, :], ACT.Gelu,
                                             bias=bias_t[:, bass.ds(col, 1)]).then_inc(hid_done, 1)

            steps_of(act, step)

        @block.vector
        def _(dve):
            steps = [0]

            def link(ins):
                steps[0] += 1
                ins.then_inc(chain, 1)
                dve.wait_ge(chain, steps[0])

            nc.vector.memset(xf[:, :, :, 0, :], 0.0).then_inc(x_zero, 1)
            for n, v in enumerate((0.25, 0.0)):
                part = slice(n * N, (n + 1) * N)
                nc.vector.memset(phase[part, 0:1], v)
                nc.vector.memset(phase[part, 1:2], v + 0.25)
                nc.vector.memset(phase[part, 2:3], v * TURN)
                last = nc.vector.memset(phase[part, 3:4], (v + 0.25) * TURN)
            link(last)

            s = [small[:, n, :] for n in range(18)]
            c_re, c_im = ccs[:, :, 0], ccs[:, :, 1]
            TT, TS, STT = nc.vector.tensor_tensor, nc.vector.tensor_scalar, nc.vector.scalar_tensor_tensor
            whole, rem, poly = tiny[:, 0:1], tiny[:, 1:2], tiny[:, 2:3]
            dve.wait_ge(in_ld, 16)
            link(TS(whole, ld[:], 1.0 / math.log(2.0), MAGIC, ALU.mult, ALU.add))
            link(TS(whole, whole, -MAGIC, -126.0, ALU.add, ALU.max))
            link(STT(rem, whole, -LN2_HI, ld[:], ALU.mult, ALU.add))
            link(STT(rem, whole, -LN2_LO, rem, ALU.mult, ALU.add))
            TS(power[:], whole, 127.0, 2.0 ** 23, ALU.add, ALU.mult)
            link(TS(poly, rem, 1.0 / math.factorial(7), None, ALU.mult))
            for n in range(6, 0, -1):
                link(STT(poly, poly, 1.0 / math.factorial(n), rem, ALU.add, ALU.mult))
            link(STT(dt_c[:], poly, 1.0, power[:].bitcast(F32), ALU.add, ALU.mult))
            dve.wait_ge(in_ai, 32)
            dve.wait_ge(abs_done, 1)
            TS(s[1], s[0], dt_c[:], -1.0, ALU.mult, ALU.mult)
            link(TS(s[2], ai[:], dt_c[:], INV_TURN, ALU.mult, ALU.mult))
            TS(s[8], s[2], 0.5, MAGIC, ALU.mult, ALU.add)
            link(TS(s[10], s[2], 0.5, 0.25, ALU.mult, ALU.add))
            TS(s[9], s[10], MAGIC, -MAGIC, ALU.add, ALU.add)
            link(TS(s[8], s[8], -MAGIC, None, ALU.add))
            STT(s[3], s[2], 0.5, s[8], ALU.mult, ALU.subtract)
            TT(s[4], s[10], s[9], ALU.subtract).then_inc(red_half, 1)
            TT(s[11], s[0], s[0], ALU.mult)
            link(TT(s[12], ai[:], ai[:], ALU.mult))
            link(TT(s[11], s[11], s[12], ALU.add))
            link(nc.vector.reciprocal(s[11], s[11]))
            dve.wait_ge(sin_half, 2)
            link(TS(s[12], s[5], -1.0, 1.0, ALU.mult, ALU.add))
            link(nc.vector.reciprocal(s[12], s[12]))
            STT(s[13], s[5], 2.0, s[12], ALU.mult, ALU.mult)
            STT(s[14], s[6], 2.0, s[6], ALU.mult, ALU.mult)
            link(STT(s[15], s[6], 2.0, s[7], ALU.mult, ALU.mult))
            TS(s[12], s[14], -1.0, 1.0, ALU.mult, ALU.add)
            link(STT(s[16], s[13], 1.0, s[15], ALU.add, ALU.mult))
            link(TT(s[12], s[13], s[12], ALU.mult))
            link(TT(s[12], s[12], s[14], ALU.subtract))
            TT(s[13], c_re, s[12], ALU.mult)
            TT(s[14], c_im, s[16], ALU.mult)
            TT(s[15], c_re, s[16], ALU.mult)
            link(TT(s[17], c_im, s[12], ALU.mult))
            TT(s[13], s[13], s[14], ALU.subtract)
            link(TT(s[15], s[15], s[17], ALU.add))
            TT(s[12], s[13], s[0], ALU.mult)
            TT(s[14], s[15], ai[:], ALU.mult)
            TT(s[16], s[13], ai[:], ALU.mult)
            link(TT(s[17], s[15], s[0], ALU.mult))
            TT(s[14], s[14], s[12], ALU.subtract)
            link(TT(s[16], s[16], s[17], ALU.add))
            for n in range(2):
                part = slice(n * N, (n + 1) * N)
                sign = 1.0 - 2.0 * n
                nc.vector.tensor_copy(stack[:, 0, part], s[2])
                nc.vector.tensor_copy(stack[:, 1, part], s[1])
                STT(stack[:, 2, part], s[14], 2.0 * sign, s[11], ALU.mult, ALU.mult)
                STT(stack[:, 3, part], s[16], -2.0 * sign, s[11], ALU.mult, ALU.mult).then_inc(stack_done, 1)

            dve.wait_ge(iota_done, 7)
            link(nc.vector.tensor_copy(exps[:], exps_i[:]))
            dve.wait_ge(par_t, 1)
            nc.vector.tensor_copy(par[:], ps_h[:, 1, 0, 0:4 * C].rearrange("p (q h) -> p q h", q=4)
                                  ).then_inc(par_done, 1)
            dve.wait_ge(par_done, 1)

            first = AHEAD * QUAD
            TT(mag[:, :, 0:first, :], par[:, 1, 0:first].unsqueeze(1).unsqueeze(3).to_broadcast([P, 2, first, RAD]),
               exps[:].unsqueeze(2).to_broadcast([P, 2, first, RAD]), ALU.mult).then_inc(mag_arg, 1)

            MAKER = 5

            def angles(j):
                own = par[:, 0, bass.ds(j * QUAD, QUAD)]
                need(dve, e_done, j * 1)
                TT(turns[:], own.unsqueeze(1).unsqueeze(3).to_broadcast([P, 2, QUAD, RAD]),
                   exps[:].unsqueeze(2).to_broadcast([P, 2, QUAD, RAD]), ALU.mult).then_inc(maker, 1)
                dve.wait_ge(maker, j * MAKER + 1)
                TS(nearest[:, 0:2], turns[:], phase[:, 0:1], MAGIC, ALU.add, ALU.add).then_inc(maker, 1)
                TS(nearest[:, 2], turns[:, 1], phase[:, 1:2], MAGIC, ALU.add, ALU.add).then_inc(maker, 1)
                dve.wait_ge(maker, j * MAKER + 2)
                STT(wave[:, 0:2], nearest[:, 0:2], MAGIC, turns[:], ALU.subtract, ALU.subtract).then_inc(wave_arg, 1)
                dve.wait_ge(maker, j * MAKER + 3)
                STT(wave[:, 2], nearest[:, 2], MAGIC, turns[:, 1], ALU.subtract, ALU.subtract).then_inc(wave_arg, 1)

            def factors(j):
                hs = bass.ds(j * QUAD, QUAD)
                dve.wait_ge(wave_done, j * 2 + 2)
                need(dve, k_done, j * 1)
                for n in (1, 2):
                    TT(wave[:, n], wave[:, n], par[:, n + 1, hs].unsqueeze(2).to_broadcast([P, QUAD, RAD]), ALU.mult
                       ).then_inc(maker, 1)
                TT(e1[:], wave[:, 0], mag[:, 0, hs, :], ALU.mult)
                dve.wait_ge(maker, j * MAKER + 5)
                TT(wave[:, 1], wave[:, 1], wave[:, 2], ALU.add).then_inc(sum_done, 1)
                dve.wait_ge(sum_done, j + 1)
                TT(e2[:], wave[:, 1], mag[:, 1, hs, :], ALU.mult).then_inc(e_done, 1)

            def finish_kernels(j):
                dve.wait_ge(k_done, j + 1)
                need(dve, k_stored, j * (16 * QUAD))
                TT(krow[:], ps_h[:, 0, 0, 0:RAD], dplace[:, bass.ds(j, 1), :].rearrange("p j b -> p (j b)"), ALU.add
                   ).then_inc(krow_done, 1)

            angles(0)
            dve.wait_ge(mag_done, 1)
            factors(0)
            dve.wait_ge(in_d, 64)
            angles(1)
            finish_kernels(0)
            factors(1)
            finish_kernels(1)

            dve.wait_ge(in_ints, 64)
            nc.vector.tensor_copy(time_rev[:], time_i[:])
            nc.vector.tensor_copy(row_t[:], row_i[:])
            nc.vector.tensor_copy(chan_of[:], chan_i[:])
            nc.vector.tensor_copy(sess_of[:], sess_i[:])
            link(nc.vector.tensor_copy(ints_f[:], ints[:]))
            TT(mask1[:], time_rev[:].unsqueeze(2).to_broadcast([P, CH, B]),
               ints_f[:, 0, :].unsqueeze(1).to_broadcast([P, CH, B]), ALU.is_lt)
            TS(onehot[:], ints_f[0:SESS, 3, :], sess_of[:], None, ALU.is_equal).then_inc(onehot_done, 1)
            for n in range(2):
                part = slice(n * C, (n + 1) * C)
                own = ints_f[part].rearrange("p v (q b) -> p v q b", b=2)
                nc.vector.tensor_copy(len2_p[part, :], own[:, 1, :, n])
                last = TS(cmask[part, :], own[:, 2, :, n], chan_of[part, :], None, ALU.is_gt)
            link(last)
            dve.wait_ge(bias_mm, 1)
            nc.vector.tensor_copy(bias_t[:], ps_h[:, 1, 1, 0:B]).then_inc(tables_done, 1)

            def split_x(i, m):
                dve.wait_ge(xh_done, i * 2 + (m + 1))
                nc.vector.tensor_tensor(
                    xl[:, m % 2], ps_t[:].rearrange("p n f -> p (n f)").rearrange("p (j h b) -> p h j b", h=2, b=B),
                    xh[:, m % 2], ALU.subtract).then_inc(xl_done, 1)

            def split_w(i, k):
                dve.wait_ge(wh_done, i * 4 + (k + 1))
                nc.vector.tensor_tensor(wl[:, k % 2, :], wf[:, k % WSLOTS, NEAR0:], wh[:, k % 2, :],
                                        ALU.subtract).then_inc(wl_done, 1)

            def keep_y(i, k):
                dve.wait_ge(conv_done, i * 4 + (k + 1))
                nc.vector.tensor_tensor(
                    y[:, :, :, :, bass.ds(i * 4 + k, 1)].rearrange("p q i b c -> p i q (b c)"),
                    ps_y[:, k % 2, :].rearrange("p (i q b) -> p i q b", i=CH, b=2),
                    mask1[:].rearrange("p i (q b) -> p i q b", b=2), ALU.mult).then_inc(y_done, 1)

            split_x(0, 0)
            split_w(0, 0)
            dve.wait_ge(k_pad, 16)

            def body1(i):
                for m in range(2):
                    if not (isinstance(i, int) and i == 0 and m == 0):
                        keep_y(i, 2 * m - 1)
                    split_w(i, 2 * m + 1)
                    if m == 0 and makes(i):
                        if isinstance(i, int) and i == 0:
                            dve.wait_ge(mag_done, 2)
                        angles(i + AHEAD)
                    if makes(i) or 2 * i + m + 1 < PAIRS:
                        split_x(i, m + 1)
                    if m == 1 and makes(i):
                        finish_kernels(i + AHEAD)
                    keep_y(i, 2 * m)
                    if m == 0 and makes(i):
                        factors(i + AHEAD)
                    if makes(i) or 2 * i + m + 1 < PAIRS:
                        split_w(i, 2 * m + 2)

            rounds_of(dve, body1)
            keep_y(BODIES - 1, 3)

            for t in (wbh, wbl):
                for b in range(2):
                    nc.vector.memset(t[(1 - b) * C:(2 - b) * C, :, b, :].bitcast(F32), 0.0).then_inc(wb_zero, 1)

            def split_sess(i, m):
                dve.wait_ge(wbh_done, i * 4 + (2 * m + 2))
                q = i * 2 + m
                for b in range(2):
                    part = slice(b * C, (b + 1) * C)
                    last = nc.vector.scalar_tensor_tensor(
                        wbl[part, m % 2, b, :], wg[part, m % 2, :], cmask[part, bass.ds(q, 1)],
                        wbh[part, m % 2, b, :], ALU.mult, ALU.subtract)
                last.then_inc(wbl_done, 1)

            def step(i, k):
                hf = k % 2
                half = slice(hf * HALF, (hf + 1) * HALF)
                if exists(i, k + 2):
                    m = ((k + 2) // 2) % 2
                    dve.wait_ge(t2_done, i * 4 + (k + 3))
                    if k % 2 == 0:
                        dve.wait_ge(xn_loaded[m], i * 16 + (16 * ((k + 2) // 4) + 16))
                    need(dve, out_done, i * 4 + (k - 1))
                    nc.vector.tensor_tensor(
                        xc[:, m, half].rearrange("p (i t) -> p i t", t=P),
                        ps_t[:, hf, :].rearrange("p (i t) -> p i t", t=P)[:, :, ::-1],
                        xin[:, m, half].rearrange("p (i t) -> p i t", t=P), ALU.add).then_inc(xc_done, 1)
                if isinstance(i, int) and 4 * i + k == -2:
                    split_sess(0, 0)
                if exists(i, k) and k % 2 == 0 and exists(i, k + 2):
                    split_sess(i, k // 2 + 1)
                if exists(i, k):
                    need(dve, z_done, i * 4 + (k - 1))
                    q = i * 2 + k // 2
                    nc.vector.tensor_scalar(tmask[:, hf, :], row_t[:, half], len2_p[:, bass.ds(q, 1)], None,
                                            ALU.is_lt).then_inc(tmask_done, 1)
                if exists(i, k + 2):
                    m = ((k + 2) // 2) % 2
                    dve.wait_ge(xch_done, i * 4 + (k + 3))
                    nc.vector.tensor_tensor(xcl[:, hf, :], xc[:, m, half], xch[:, hf, :],
                                            ALU.subtract).then_inc(xcl_done, 1)
                if exists(i, k):
                    m = (k // 2) % 2
                    dve.wait_ge(mm2_done, i * 4 + (k + 1))
                    dve.wait_ge(tmask_done, i * 4 + (k + 1))
                    if hf == 0:
                        need(dve, stored[m], i * 16 + 0)
                    nc.vector.scalar_tensor_tensor(z[:, m, half], ps_y[:, hf, :], b2_col[:], tmask[:, hf, :],
                                                   ALU.add, ALU.mult).then_inc(z_done, 1)

            dve.wait_ge(in_late, 64)
            steps_of(dve, step)

        @block.tensor
        def _(pe):
            def transpose_x(i, m):
                pe.wait_ge(x_loaded[m % 2], i * 32 + (32 * (m // 2) + 32))
                need(pe, xl_done, i * 2 + m)
                for j in range(CH):
                    last = nc.tensor.transpose(ps_t[:, j // 4, (j % 4) * P:(j % 4 + 1) * P],
                                               xin[:, m % 2, j * P:(j + 1) * P], ident[:])
                last.then_inc(xt_done, 1)

            def kernels(j):
                pe.wait_ge(e_done, j + 1)
                need(pe, krow_done, j * 1)
                for q in range(QUAD):
                    last = nc.tensor.matmul(ps_h[RAD * q:RAD * (q + 1), 0, 0, 0:RAD], e2[:, q, :], e1[:, q, :],
                                            start=True, stop=True)
                last.then_inc(k_done, 1)

            pe.wait_ge(ident_done, 2)
            transpose_x(0, 0)
            pe.wait_ge(stack_done, 2)
            for q in range(4):
                last = nc.tensor.transpose(ps_h[:, 1, 0, q * C:(q + 1) * C], stack[:, q, :], ident[0:C, 0:C])
            last.then_inc(par_t, 1)
            kernels(0)
            kernels(1)
            pe.wait_ge(onehot_done, 1)
            pe.wait_ge(in_late, 64)
            nc.tensor.matmul(ps_h[:, 1, 1, 0:B], bs[:], onehot[:], start=True, stop=True).then_inc(bias_mm, 1)

            def conv(i, k):
                n, h, xs = k % 2, k % 2, (k // 2) % 2
                pe.wait_ge(wl_done, i * 4 + (k + 1))
                pe.wait_ge(xl_done, i * 2 + (k // 2 + 1))
                need(pe, y_done, i * 4 + (k - 1))
                for d in range(FAR):
                    cols = slice(T - NEAR0 - P * (d + 1), T - NEAR0 - P * d)
                    for t, (w, v) in enumerate(((wh, xh), (wh, xl), (wl, xh))):
                        nc.tensor.matmul(ps_y[:, n, d * B:], w[:, n, cols], v[:, xs, h, 0:CH - d, :],
                                         start=(d == 0 and t == 0), stop=False)
                for d in range(FAR, CH):
                    first = min(d, CH - 2)
                    last = nc.tensor.matmul(ps_y[:, n, first * B:], wf[:, k % WSLOTS, T - P * (d + 1):T - P * d],
                                            xf[:, xs, h, 1 + first - d:1 + CH - d, :], start=False, stop=(d == CH - 1))
                last.then_inc(conv_done, 1)

            pe.wait_ge(x_zero, 1)

            def body1(i):
                for m in range(2):
                    if makes(i) or 2 * i + m + 1 < PAIRS:
                        transpose_x(i, m + 1)
                    conv(i, 2 * m)
                    conv(i, 2 * m + 1)
                    if m == 0 and makes(i):
                        kernels(i + AHEAD)

            rounds_of(pe, body1)

            pe.wait_ge(xl_done, PAIRS)
            pe.wait_ge(y_done, C)

            def step(i, k):
                if exists(i, k + 2):
                    hf, m = k % 2, ((k + 2) // 2) % 2
                    if hf == 0:
                        pe.wait_ge(ys_loaded[m], i * 16 + (16 * ((k + 2) // 4) + 16))
                    need(pe, xc_done, i * 4 + (k + 1))
                    for j in range(4):
                        last = nc.tensor.transpose(ps_t[:, hf, j * P:(j + 1) * P], ys[:, m, 4 * hf + j, :], ident[:])
                    last.then_inc(t2_done, 1)
                if exists(i, k + 1):
                    hf, m = (k + 1) % 2, ((k + 1) // 2) % 2
                    pe.wait_ge(xcl_done, i * 4 + (k + 2))
                    pe.wait_ge(wbl_done, i * 2 + ((k + 1) // 2 + 1))
                    need(pe, hid_done, i * 8 + 2 * k)
                    for b in range(2):
                        for t, (w, v) in enumerate(((wbh, xch), (wbh, xcl), (wbl, xch))):
                            last = nc.tensor.matmul(ps_h[:, hf, b, :], w[:, m, b, :], v[:, hf, :],
                                                    start=(t == 0), stop=(t == 2))
                    last.then_inc(mm1_done, 1)
                if exists(i, k):
                    hf = k % 2
                    pe.wait_ge(hid_done, i * 8 + (2 * k + 2))
                    need(pe, z_done, i * 4 + (k - 1))
                    for b in range(2):
                        last = nc.tensor.matmul(ps_y[b * C:(b + 1) * C, hf, :], w2_s[:], hid[:, hf, b, :],
                                                start=True, stop=True)
                    last.then_inc(mm2_done, 1)

            steps_of(pe, step)


_INS = ["x", "itok_B_78_3631", "itok_B_0_7", "itok_B_2182_4065", "_lenS", "L0_cond_log_dt", "L0_cond_C",
        "L0_cond_log_A_real", "L0_cond_A_imag", "L0_cond_D", "L1_cond_W_sess", "L1_cond_b_sess", "L1_cond_W2",
        "L1_cond_b2"]


def kernel(**inputs):
    import numpy as np
    import concourse.bacc as bacc
    from concourse.bass_utils import run_bass_kernel_spmd

    nc = bacc.Bacc("TRN2", target_bir_lowering=False, num_devices=1, dynamic_dma_scratch_size=8192)
    arrays, args = {}, []
    for name in _INS:
        a = np.ascontiguousarray(inputs[name])
        arrays[f"in_{name}"] = a
        args.append(nc.dram_tensor(f"in_{name}", a.shape, mybir.dt.from_np(a.dtype), kind="ExternalInput").ap())
    args.append(nc.dram_tensor("out_0", (B, C, T), F32, kind="ExternalOutput").ap())
    x, len1, sid, len2, chans, log_dt, cc, log_a, a_imag, dskip, w_sess, b_sess, w2, b2, out = args
    build_program(nc, x, len1, sid, len2, chans, log_dt, cc, log_a, a_imag, dskip, w_sess, b_sess, w2, b2, out)
    r = run_bass_kernel_spmd(nc, [arrays], core_ids=[0])
    return r.results[0]["out_0"]
```

```python
import math
from contextlib import ExitStack

import concourse.bass as bass
from concourse import mybir

F32 = mybir.dt.float32
F32R = mybir.dt.float32r
I32 = mybir.dt.int32
F16 = mybir.dt.float16
ALU = mybir.AluOpType
ACT = mybir.ActivationFunctionType

B, C, T = 64, 64, 1024
N = 64
HID, SESS = 128, 8
P = 128
HALF = T // 2
CH = T // P
DUOS = CH // 2
SPLIT = CH - 3
RAD = 32
KPAD = T + P
QUAD = 4
ROUNDS = C // QUAD
AHEAD = 2
GROUP = 8
BODIES = C // GROUP
PAIRS = C // 2
PG = GROUP // 2
STEPS = 2 * PAIRS
LEAD = 3
MAGIC = 1.5 * 2.0 ** 23
TURN = 6.283185
INV_TURN = 1.0 / (2.0 * math.pi)
LN2_HI = 0.693359375
LN2_LO = math.log(2.0) - LN2_HI


def need(eng, sem, value):
    if isinstance(value, int) and value <= 0:
        return
    eng.wait_ge(sem, value)


def build_program(nc, x, len1, sid, len2, chans, log_dt, cc, log_a, a_imag, dskip, w_sess, b_sess, w2, b2, out):
    kr = nc.dram_tensor("kr", (C, KPAD), F32, kind="Internal").ap()
    xcd = nc.dram_tensor("xcd", (B, C, T), F32, kind="Internal").ap()
    wsd = nc.dram_tensor("wsd", (SESS, C, 2, HID), F32, kind="Internal").ap()
    xc_rows = xcd.rearrange("b c t -> (b c) t")
    out_rows = out.rearrange("b c t -> (b c) t")
    toeplitz = bass.AP(kr.tensor, 0, [[KPAD, C], [1, P], [1, T]])

    def chunk_rows(rows, q, h, g):
        view = bass.AP(rows.tensor, 0, [[2 * T, PAIRS], [T, 2], [P, 2], [C * T, B], [2 * P, DUOS], [1, P]])
        return view[bass.ds(q, 1), h, g ^ h].rearrange("q b m t -> (q b) m t")

    ctx = ExitStack()
    with ctx:
        def sb(name, shape, dt=F32):
            return ctx.enter_context(nc.sbuf_tensor(name, shape, dt))

        def sem(name):
            return ctx.enter_context(nc.semaphore(name))

        ident = sb("ident", [P, P])
        row_t = sb("row_t", [P, T], F16)
        len1_i = sb("len1_i", [P, 1], I32)
        duo_t = sb("duo_t", [P, DUOS, P], F16)
        limit = sb("limit", [P, 2])
        sids = sb("sids", [1, B], I32)
        cols = sb("cols", [P, PAIRS, 4])
        w2_s = sb("w2_s", [HID, C])
        b2_col = sb("b2_col", [P, 1])
        ones = sb("ones", [P, P])
        duo_i = sb("duo_i", [P, DUOS, P], I32)
        chan_i = sb("chan_i", [P, 1], I32)
        chan_of = sb("chan_of", [P, 1])
        ints = sb("ints", [P, 3, B], I32)
        ints_f = sb("ints_f", [P, 3, B])
        sess_i = sb("sess_i", [SESS, 1], I32)
        sess_of = sb("sess_of", [SESS, 1])
        onehot = sb("onehot", [SESS, B])
        bs = sb("bs", [SESS, HID])
        la = sb("la", [C, N])
        ai = sb("ai", [C, N])
        ccs = sb("ccs", [C, N, 2])
        ld = sb("ld", [C, 1])
        power = sb("power", [C, 1], I32)
        tiny = sb("tiny", [C, 4])
        dt_c = sb("dt_c", [C, 1])
        small = sb("small", [C, 18, N])
        stack = sb("stack", [C, 4, P])
        zrow = sb("zrow", [C, P])
        exps_i = sb("exps_i", [P, 2, RAD], I32)
        exps = sb("exps", [P, 2, RAD])
        par = sb("par", [P, 4, C])
        phase = sb("phase", [P, 4])
        mag = sb("mag", [P, 2, C, RAD])
        turns = sb("turns", [P, 2, QUAD, RAD])
        nearest = sb("nearest", [P, 3, QUAD, RAD])
        wave = sb("wave", [P, 3, QUAD, RAD])
        e1 = sb("e1", [P, QUAD, RAD])
        e2 = sb("e2", [P, QUAD, RAD])
        dplace = sb("dplace", [P, ROUNDS, RAD])
        krow = sb("krow", [P, RAD])
        xin = sb("xin", [P, PG, 2, DUOS, P])
        wf = sb("wf", [P, GROUP, T])
        wh = sb("wh", [P, 4, T], F32R)
        wl = sb("wl", [P, 4, T], F32R)
        xh = sb("xh", [P, 2, 2, CH * B], F32R)
        xl = sb("xl", [P, 2, 2, CH * B], F32R)
        xf = sb("xf", [P, 2, 2, CH * B])
        yst = sb("yst", [P, 2, 2, DUOS, P])
        xc = sb("xc", [P, PG, T])
        xch = sb("xch", [P, 4, HALF], F32R)
        xcl = sb("xcl", [P, 4, HALF], F32R)
        hid = sb("hid", [P, 2, 2, HALF])
        tmask = sb("tmask", [P, 2, HALF], F16)
        z = sb("z", [P, 2, T])
        cols_p = sb("cols_p", [P, PG, 4])
        wb = sb("wb", [P, PG, 2, 2, HID], F32R)
        row_i = xc[:, PG - 1, :].bitcast(I32)
        ws = xc[0:C, 0, :].rearrange("c (s n) -> c s n", n=HID)
        ws_parts = xc[0:C, 1:3, :].bitcast(F32R).rearrange("c v (s n) -> c s v n", n=HID)

        ps_t = ctx.enter_context(nc.psum_tensor("ps_t", [P, 2, 512], F32))
        ps_y = ctx.enter_context(nc.psum_tensor("ps_y", [P, 4, 512], F32))
        ps_k = ctx.enter_context(nc.psum_tensor("ps_k", [P, 2, 512], F32))
        ps_o = ps_t
        ps_h = ps_y[:].rearrange("p (s b) t -> p s b t", b=2)

        in_ld = sem("in_ld")
        in_la = sem("in_la")
        in_ai = sem("in_ai")
        in_len1 = sem("in_len1")
        in_ints = sem("in_ints")
        in_sids = sem("in_sids")
        in_late = sem("in_late")
        in_d = sem("in_d")
        ident_done = sem("ident_done")
        iota_done = sem("iota_done")
        exps_done = sem("exps_done")
        d_zero = sem("d_zero")
        chain = sem("chain")
        abs_done = sem("abs_done")
        red_half = sem("red_half")
        sin_half = sem("sin_half")
        stack_done = sem("stack_done")
        par_t = sem("par_t")
        par_done = sem("par_done")
        mag_arg = [sem(f"mag_arg{n}") for n in range(2)]
        mag_done = sem("mag_done")
        maker = sem("maker")
        wave_arg = sem("wave_arg")
        wave_done = sem("wave_done")
        sum_done = sem("sum_done")
        e_done = sem("e_done")
        k_done = sem("k_done")
        krow_done = sem("krow_done")
        k_pad = sem("k_pad")
        k_stored = sem("k_stored")
        onehot_done = sem("onehot_done")
        bias_mm = sem("bias_mm")
        limit_done = sem("limit_done")
        tables_done = sem("tables_done")
        x_loaded = [sem(f"x_loaded{n}") for n in range(PG)]
        w_loaded = [sem(f"w_loaded{n}") for n in range(PG)]
        w_first = sem("w_first")
        first_rows = sem("first_rows")
        next_rows = sem("next_rows")
        late_rows = sem("late_rows")
        xt_done = sem("xt_done")
        xh_done = sem("xh_done")
        xl_done = sem("xl_done")
        wh_done = sem("wh_done")
        wl_done = sem("wl_done")
        conv_done = sem("conv_done")
        y_done = sem("y_done")
        x_added = sem("x_added")
        last_added = sem("last_added")
        y_last = sem("y_last")
        y_stored = [sem(f"y_stored{n}") for n in range(2)]
        xc_loaded = [sem(f"xc_loaded{n}") for n in range(PG)]
        wb_loaded = [sem(f"wb_loaded{n}") for n in range(PG)]
        wb_zero = sem("wb_zero")
        in_ws = sem("in_ws")
        ws_upper = sem("ws_upper")
        ws_done = sem("ws_done")
        ws_stored = sem("ws_stored")
        cols_done = sem("cols_done")
        xch_done = sem("xch_done")
        xcl_done = sem("xcl_done")
        mm1_done = sem("mm1_done")
        hid_done = sem("hid_done")
        mm2_done = sem("mm2_done")
        tmask_done = sem("tmask_done")
        z_done = sem("z_done")
        out_done = sem("out_done")
        last_out = sem("last_out")
        stored = [sem(f"stored{n}") for n in range(2)]

        block = ctx.enter_context(nc.Block())

        def bodies_of(eng, body):
            body(0)
            with eng.Fori(1, BODIES - 1) as i:
                body(i)
            body(BODIES - 1)

        def steps_of(eng, step):
            for k in range(GROUP - LEAD, GROUP):
                step(-1, k)
            for k in range(GROUP):
                step(0, k)
            with eng.Fori(1, BODIES - 1) as i:
                for k in range(GROUP):
                    step(i, k)
            for k in range(GROUP):
                step(BODIES - 1, k)

        def makes(i):
            return not isinstance(i, int) or i < BODIES - 1

        def pair_exists(i, k):
            return not isinstance(i, int) or PG * i + k < PAIRS

        def exists(i, k):
            return not isinstance(i, int) or 0 <= GROUP * i + k < STEPS

        MAKER = 5

        def angles(eng, own_engine, j):
            TT, TS = own_engine.tensor_tensor, own_engine.tensor_scalar
            own = par[:, 0, bass.ds(j * QUAD, QUAD)]
            need(eng, e_done, j * 1)
            TT(turns[:], own.unsqueeze(1).unsqueeze(3).to_broadcast([P, 2, QUAD, RAD]),
               exps[:].unsqueeze(2).to_broadcast([P, 2, QUAD, RAD]), ALU.mult).then_inc(maker, 1)
            eng.wait_ge(maker, j * MAKER + 1)
            TS(nearest[:, 0:2], turns[:], phase[:, 0:1], MAGIC, ALU.add, ALU.add).then_inc(maker, 1)
            TS(nearest[:, 2], turns[:, 1], phase[:, 1:2], MAGIC, ALU.add, ALU.add).then_inc(maker, 1)

        first_channels, other_channels = slice(0, AHEAD * QUAD), slice(AHEAD * QUAD, C)

        def decay_arguments(own_engine, n):
            own = (first_channels, other_channels)[n]
            count = own.stop - own.start
            own_engine.tensor_tensor(
                mag[:, :, own, :], par[:, 1, own].unsqueeze(1).unsqueeze(3).to_broadcast([P, 2, count, RAD]),
                exps[:].unsqueeze(2).to_broadcast([P, 2, count, RAD]), ALU.mult).then_inc(mag_arg[n], 1)

        @block.sync
        def _(sp):
            sp.dma_start(ld[:], log_dt.rearrange("(h a) -> h a", a=1)).then_inc(in_ld, 16)
            sp.dma_start(la[:], log_a).then_inc(in_la, 16)

            def load_w(i, k):
                if k % 2 == 0:
                    sp.wait_ge(k_stored, i * 32 + (16 * (k // 2) + 16))
                src = toeplitz[bass.ds(i * GROUP + 2 * k, 2)].rearrange("h s c -> s h c")
                sp.dma_start(wf[:, 2 * (k % PG):2 * (k % PG) + 2, :], src).then_inc(w_loaded[k % PG], 16)

            def store_kernels(j):
                sp.wait_ge(krow_done, j + 1)
                sp.dma_start(kr[bass.ds(j * QUAD, QUAD), 0:T].rearrange("h (a b) -> h a b", b=RAD),
                             krow[:]).then_inc(k_stored, 16)

            def store_channel(i, k, h):
                last = isinstance(i, int) and i == BODIES - 1 and k == PG - 1
                if last and h == 1:
                    sp.wait_ge(last_added, 1)
                else:
                    sp.wait_ge(x_added, i * GROUP + (2 * k + h + 1))
                for g in range(2):
                    sp.dma_start(chunk_rows(xcd, i * PG + k, h, g), yst[g * B:(g + 1) * B, k % 2, h]
                                 ).then_inc(y_last if last else y_stored[k % 2], 16)

            def store_y(i, k):
                for h in range(2):
                    store_channel(i, k, h)

            def load_weights(i, k):
                for b in range(2):
                    s = sp.value_load(sids[0:1, bass.ds(i * GROUP + (2 * k + b), 1)], min_val=0, max_val=SESS - 1)
                    sp.dma_start(wb[b * C:(b + 1) * C, k % PG, b, :, :].bitcast(F32),
                                 wsd[bass.ds(s, 1)].rearrange("s c v n -> (s c) v n")).then_inc(wb_loaded[k % PG], 16)

            def load_first_x(k):
                for h in range(2):
                    for g in range(2):
                        sp.dma_start(xin[g * B:(g + 1) * B, k, h], chunk_rows(x, k, h, g)).then_inc(x_loaded[k], 16)

            load_first_x(0)
            sp.wait_ge(d_zero, 1)
            for q in range(QUAD):
                sp.dma_start(dplace[RAD * (q + 1) - 1:RAD * (q + 1), :, RAD - 1:RAD],
                             bass.AP(dskip.tensor, q, [[C, 1], [QUAD, ROUNDS], [1, 1]]),
                             allow_slow_non_contiguous=True).then_inc(in_d, 16)
            sp.dma_start(kr[:, T:KPAD], zrow[:]).then_inc(k_pad, 16)
            sp.dma_start(len1_i[:], bass.AP(len1.tensor, 0, [[0, 2], [1, B], [1, 1]])).then_inc(in_len1, 16)
            load_first_x(1)
            sp.wait_ge(k_pad, 16)

            store_kernels(0)
            sp.wait_ge(k_stored, 16)
            sp.dma_start(wf[:, 0, :], toeplitz[0]).then_inc(w_first, 16)
            sp.dma_start(wf[:, 1, :], toeplitz[1]).then_inc(w_loaded[0], 16)
            load_w(0, 1)
            store_kernels(1)
            load_first_x(2)
            for n, v in enumerate((len2, chans, sid)):
                sp.dma_start(ints[:, n, :], bass.AP(v.tensor, 0, [[0, P], [1, B]])).then_inc(in_ints, 16)
            sp.dma_start(sids[:], sid.rearrange("(a b) -> a b", a=1)).then_inc(in_sids, 16)
            sp.dma_start(bs[:], b_sess).then_inc(in_late, 16)
            sp.dma_start(w2_s[:], w2).then_inc(in_late, 16)
            sp.dma_start(b2_col[:], bass.AP(b2.tensor, 0, [[0, 2], [1, C], [1, 1]])).then_inc(in_late, 16)
            sp.dma_start(ws, w_sess.rearrange("s c n -> c s n")).then_inc(in_ws, 16)

            def body1(i):
                for k in range(PG):
                    if isinstance(i, int) and i == 0 and k == PG - 1:
                        sp.wait_ge(ws_done, 1)
                        for v in range(2):
                            sp.dma_start(wsd[:, :, v, :].rearrange("s c n -> c s n"), ws_parts[:, :, v, :].bitcast(F32)
                                         ).then_inc(ws_stored, 16)
                        sp.wait_ge(in_sids, 16)
                    if isinstance(i, int) and i == BODIES - 1 and k == PG - 2:
                        sp.wait_ge(ws_stored, 32)
                        for n in range(PG):
                            load_weights(0, n)
                    if pair_exists(i, k + 2):
                        load_w(i, k + 2)
                    if not (isinstance(i, int) and (i == 0 and k == 0 or i == BODIES - 1 and k == PG - 1)):
                        store_y(i - (k == 0), (k - 1) % PG)
                    if k % 2 == 1 and makes(i):
                        store_kernels(i * 2 + (k // 2 + AHEAD))

            bodies_of(sp, body1)
            store_y(BODIES - 1, PG - 2)
            xc_pairs = xc_rows.rearrange("(q b c) t -> b c q t", b=2, c=C)

            def load_rows(b, channels, pairs, done):
                sp.dma_start(xc[b * C + channels.start:b * C + channels.stop, pairs, :], xc_pairs[b, channels, pairs, :]
                             ).then_inc(done, 16)

            last_two = slice(C - 2, C)
            store_y(BODIES - 1, PG - 1)
            sp.wait_ge(y_stored[0], 64 * (PAIRS // 2))
            sp.wait_ge(y_stored[1], 64 * (PAIRS // 2 - 1))
            for b in range(2):
                load_rows(b, slice(0, C - 2), slice(0, 1), first_rows)
            sp.wait_ge(y_last, 64)
            for b in range(2):
                load_rows(b, last_two, slice(0, PG - 1), late_rows)
            for b in range(2):
                load_rows(b, slice(0, C - 2), slice(1, PG - 1), next_rows)

            def load_pair(i, k):
                need(sp, out_done, i * GROUP + (2 * (k - PG) + 2))
                sp.dma_start(xc[:, k % PG, :], xc_rows[bass.ds(i * (PG * P) + k * P, P), :]
                             ).then_inc(xc_loaded[k % PG], 16)

            def store_pair(i, k):
                sp.wait_ge(out_done, i * GROUP + (2 * k + 2))
                sp.dma_start(out_rows[bass.ds(i * (PG * P) + k * P, P), :], z[:, k % 2, :]
                             ).then_inc(stored[k % 2], 16)

            load_pair(0, PG - 1)

            def body2(i):
                for k in range(PG):
                    if pair_exists(i, k + PG):
                        load_pair(i, k + PG)
                    if pair_exists(i, k + 1):
                        store_pair(i, k)
                    if pair_exists(i, k + PG):
                        load_weights(i, k + PG)

            bodies_of(sp, body2)
            for n in range(2):
                sp.wait_ge(out_done if n == 0 else last_out, STEPS - 1 if n == 0 else 1)
                half = slice(n * HALF, (n + 1) * HALF)
                sp.dma_start(out_rows[(PAIRS - 1) * P:PAIRS * P, half], z[:, 1, half]).then_inc(stored[1 - n], 16)
            sp.wait_ge(stored[0], 16 * (PAIRS // 2 + 1))
            sp.wait_ge(stored[1], 16 * (PAIRS // 2))

        @block.gpsimd
        def _(pool):
            nc.gpsimd.memset(dplace[:], 0.0)
            nc.gpsimd.memset(zrow[:], 0.0).then_inc(d_zero, 1)
            nc.gpsimd.memset(ones[:], 1.0).then_inc(ident_done, 1)
            pool.wait_ge(ident_done, 1)
            nc.gpsimd.affine_select(out=ident[:], in_=ones[:], compare_op=ALU.is_equal, fill=0.0, base=0,
                                    pattern=[[-1, P]], channel_multiplier=1).then_inc(ident_done, 1)
            nc.gpsimd.iota(exps_i[:, 0, :], pattern=[[-1, RAD]], base=RAD - 1, channel_multiplier=0).then_inc(iota_done, 1)
            nc.gpsimd.iota(exps_i[:, 1, :], pattern=[[-RAD, RAD]], base=RAD * (RAD - 1),
                           channel_multiplier=0).then_inc(iota_done, 1)
            nc.gpsimd.iota(duo_i[:], pattern=[[2 * P, DUOS], [1, P]], base=0, channel_multiplier=0).then_inc(iota_done, 1)
            nc.gpsimd.iota(row_i, pattern=[[1, T]], base=0, channel_multiplier=0).then_inc(iota_done, 1)
            for n in range(2):
                pool.wait_ge(iota_done, 4 + n)
                nc.gpsimd.iota(chan_i[n * C:(n + 1) * C, :], pattern=[[0, 1]], base=0,
                               channel_multiplier=1).then_inc(iota_done, 1)
            pool.wait_ge(iota_done, 6)
            nc.gpsimd.iota(sess_i[:], pattern=[[0, 1]], base=0, channel_multiplier=1).then_inc(iota_done, 1)

            pool.wait_ge(iota_done, 2)
            nc.gpsimd.tensor_copy(exps[:], exps_i[:]).then_inc(exps_done, 1)
            pool.wait_ge(exps_done, 1)
            pool.wait_ge(par_done, 1)
            pool.wait_ge(chain, 1)
            angles(pool, nc.gpsimd, 0)
            decay_arguments(nc.gpsimd, 1)

            pool.wait_ge(mag_arg[1], 1)
            for b in range(2):
                nc.gpsimd.memset(wb[(1 - b) * C:(2 - b) * C, :, b, :, :].bitcast(F32), 0.0).then_inc(wb_zero, 1)
                pool.wait_ge(wb_zero, b + 1)

            def body1(i):
                for k in range(GROUP):
                    if isinstance(i, int) and i == BODIES - 1 and k == GROUP - 1:
                        break
                    pool.wait_ge(y_done, i * GROUP + (k + 1))
                    own = yst[:, (k // 2) % 2, k % 2]
                    nc.gpsimd.tensor_tensor(own, own, xin[:, k // 2, k % 2], ALU.add).then_inc(x_added, 1)

            bodies_of(pool, body1)

            def body2(i):
                for k in range(GROUP):
                    if isinstance(i, int) and i == BODIES - 1 and k == GROUP - 1:
                        break
                    pool.wait_ge(z_done, i * GROUP + (k + 1))
                    half = slice((k % 2) * HALF, (k % 2 + 1) * HALF)
                    nc.gpsimd.tensor_tensor(z[:, (k // 2) % 2, half], z[:, (k // 2) % 2, half],
                                            xc[:, k // 2, half], ALU.add).then_inc(out_done, 1)

            bodies_of(pool, body2)

        @block.scalar
        def _(act):
            def load_x(i, k):
                need(act, x_added, i * GROUP + 2 * (k - PG + 1))
                for h in range(2):
                    for g in range(2):
                        act.dma_start(xin[g * B:(g + 1) * B, k % PG, h], chunk_rows(x, i * PG + k, h, g)
                                     ).then_inc(x_loaded[k % PG], 16)

            act.dma_start(ai[:], a_imag).then_inc(in_ai, 16)
            act.dma_start(ccs[:], cc).then_inc(in_ai, 16)
            act.wait_ge(in_la, 16)
            nc.scalar.activation(small[:, 0, :], la[:], ACT.Exp).then_inc(abs_done, 1)
            act.wait_ge(red_half, 1)
            nc.scalar.activation(small[:, 5, :], small[:, 1, :], ACT.Tanh, scale=0.5).then_inc(sin_half, 1)
            nc.scalar.activation(small[:, 6:8, :], small[:, 3:5, :], ACT.Sin, scale=TURN).then_inc(sin_half, 1)

            def waves(j):
                act.wait_ge(wave_arg, j * 2 + 1)
                nc.scalar.activation(wave[:, 0:2], wave[:, 0:2], ACT.Sin, scale=-TURN, bias=phase[:, 2:3]
                                     ).then_inc(wave_done, 1)
                act.wait_ge(wave_arg, j * 2 + 2)
                nc.scalar.activation(wave[:, 2], wave[:, 2], ACT.Sin, scale=-TURN, bias=phase[:, 3:4]
                                     ).then_inc(wave_done, 1)

            def decays(n):
                own = (first_channels, other_channels)[n]
                act.wait_ge(mag_arg[n], 1)
                nc.scalar.activation(mag[:, :, own, :], mag[:, :, own, :], ACT.Exp).then_inc(mag_done, 1)

            def split_x(i, k):
                act.wait_ge(xt_done, i * PG + (k + 1))
                need(act, conv_done, i * GROUP + (2 * k - 2))
                nc.scalar.copy(xf[:, k % 2], ps_t[:])
                nc.scalar.copy(xh[:, k % 2], ps_t[:]).then_inc(xh_done, 1)

            act.wait_ge(par_t, 1)
            nc.scalar.copy(par[:, 0:2], ps_k[:, 1, 0:2 * C].rearrange("p (q h) -> p q h", q=2)).then_inc(par_done, 1)
            decays(0)
            waves(0)
            split_x(0, 0)
            waves(1)

            def split_w(i, k):
                if isinstance(i, int) and i == 0 and k == 0:
                    act.wait_ge(w_first, 16)
                else:
                    act.wait_ge(w_loaded[(k // 2) % PG], i * 16 + (16 * (k // GROUP) + 16))
                need(act, conv_done, i * GROUP + (k // 2 * 2 - 2))
                nc.scalar.copy(wh[:, k % 4, P:], wf[:, k % GROUP, P:]).then_inc(wh_done, 1)

            for h in range(2):
                split_w(0, h)
            decays(1)

            def body1(i):
                for k in range(PG):
                    if pair_exists(i, k + 2) and not (isinstance(i, int) and i == 0 and k == 0):
                        load_x(i, k + 2)
                    if pair_exists(i, k + 1):
                        split_x(i, k + 1)
                        split_w(i, 2 * (k + 1))
                        if k % 2 == 0 and makes(i):
                            waves(i * 2 + (k // 2 + AHEAD))
                        split_w(i, 2 * (k + 1) + 1)

            bodies_of(act, body1)

            def step(i, k):
                if exists(i, k + 1):
                    n = (k + 1) % 2
                    act.wait_ge(mm1_done, i * GROUP + (k + 2))
                    need(act, mm2_done, i * GROUP + k)
                    for b in range(2):
                        nc.scalar.activation(hid[:, n, b, :], ps_h[:, n, b, :], ACT.Gelu,
                                             bias=cols_p[:, ((k + 1) // 2) % PG, b:b + 1]).then_inc(hid_done, 1)
                if exists(i, k + LEAD):
                    kk = k + LEAD
                    if kk % 2 == 0 and isinstance(i, int) and GROUP * i + kk < GROUP - 2:
                        act.wait_ge(first_rows if GROUP * i + kk == 0 else next_rows, 32)
                        act.wait_ge(late_rows, 32)
                    elif kk % 2 == 0:
                        uncounted = 16 * ((kk // 2) % PG < PG - 1)
                        act.wait_ge(xc_loaded[(kk // 2) % PG], i * 16 + (16 * (kk // GROUP) + 16 - uncounted))
                    act.wait_ge(cols_done, i * PG + (kk // 2 + 1))
                    need(act, mm1_done, i * GROUP + (kk - 3))
                    half = slice((kk % 2) * HALF, (kk % 2 + 1) * HALF)
                    nc.scalar.activation(xch[:, kk % 4, :], xc[:, (kk // 2) % PG, half], ACT.Copy,
                                         scale=cols_p[:, (kk // 2) % PG, 2:3]).then_inc(xch_done, 1)

            steps_of(act, step)

        @block.vector
        def _(dve):
            steps = [0]

            def link(ins):
                steps[0] += 1
                ins.then_inc(chain, 1)
                dve.wait_ge(chain, steps[0])

            for n, v in enumerate((0.25, 0.0)):
                part = slice(n * N, (n + 1) * N)
                nc.vector.memset(phase[part, 0:1], v)
                nc.vector.memset(phase[part, 1:2], v + 0.25)
                nc.vector.memset(phase[part, 2:3], v * TURN)
                last = nc.vector.memset(phase[part, 3:4], (v + 0.25) * TURN)
            link(last)

            s = [small[:, n, :] for n in range(18)]
            c_re, c_im = ccs[:, :, 0], ccs[:, :, 1]
            TT, TS, STT = nc.vector.tensor_tensor, nc.vector.tensor_scalar, nc.vector.scalar_tensor_tensor
            def reduce(j):
                dve.wait_ge(maker, j * MAKER + 2)
                STT(wave[:, 0:2], nearest[:, 0:2], MAGIC, turns[:], ALU.subtract, ALU.subtract).then_inc(wave_arg, 1)
                dve.wait_ge(maker, j * MAKER + 3)
                STT(wave[:, 2], nearest[:, 2], MAGIC, turns[:, 1], ALU.subtract, ALU.subtract).then_inc(wave_arg, 1)

            whole, rem, poly = tiny[:, 0:1], tiny[:, 1:2], tiny[:, 2:3]
            dve.wait_ge(in_ld, 16)
            link(TS(whole, ld[:], 1.0 / math.log(2.0), MAGIC, ALU.mult, ALU.add))
            link(TS(whole, whole, -MAGIC, -126.0, ALU.add, ALU.max))
            link(STT(rem, whole, -LN2_HI, ld[:], ALU.mult, ALU.add))
            link(STT(rem, whole, -LN2_LO, rem, ALU.mult, ALU.add))
            TS(power[:], whole, 127.0, 2.0 ** 23, ALU.add, ALU.mult)
            link(TS(poly, rem, 1.0 / math.factorial(7), None, ALU.mult))
            for n in range(6, 0, -1):
                link(STT(poly, poly, 1.0 / math.factorial(n), rem, ALU.add, ALU.mult))
            link(STT(dt_c[:], poly, 1.0, power[:].bitcast(F32), ALU.add, ALU.mult))
            dve.wait_ge(in_ai, 32)
            dve.wait_ge(abs_done, 1)
            TS(s[1], s[0], dt_c[:], -1.0, ALU.mult, ALU.mult)
            link(TS(s[2], ai[:], dt_c[:], INV_TURN, ALU.mult, ALU.mult))
            TS(s[8], s[2], 0.5, MAGIC, ALU.mult, ALU.add)
            link(TS(s[10], s[2], 0.5, 0.25, ALU.mult, ALU.add))
            TS(s[9], s[10], MAGIC, -MAGIC, ALU.add, ALU.add)
            link(TS(s[8], s[8], -MAGIC, None, ALU.add))
            STT(s[3], s[2], 0.5, s[8], ALU.mult, ALU.subtract)
            TT(s[4], s[10], s[9], ALU.subtract).then_inc(red_half, 1)
            for n in range(2):
                part = slice(n * N, (n + 1) * N)
                nc.vector.tensor_copy(stack[:, 0, part], s[2])
                nc.vector.tensor_copy(stack[:, 1, part], s[1]).then_inc(stack_done, 1)
            TT(s[11], s[0], s[0], ALU.mult)
            TT(s[12], ai[:], ai[:], ALU.mult)
            TT(s[13], c_re, s[0], ALU.mult)
            TT(s[14], c_im, ai[:], ALU.mult)
            TT(s[15], c_re, ai[:], ALU.mult)
            link(TT(s[16], c_im, s[0], ALU.mult))
            TT(s[11], s[11], s[12], ALU.add)
            TT(s[14], s[14], s[13], ALU.subtract)
            link(TT(s[15], s[15], s[16], ALU.add))
            nc.vector.reciprocal(s[11], s[11])
            dve.wait_ge(sin_half, 1)
            link(TS(s[12], s[5], -1.0, 1.0, ALU.mult, ALU.add))
            nc.vector.reciprocal(s[12], s[12])
            STT(s[17], s[14], 2.0, s[11], ALU.mult, ALU.mult)
            link(STT(s[10], s[15], -2.0, s[11], ALU.mult, ALU.mult))
            link(STT(s[13], s[5], 2.0, s[12], ALU.mult, ALU.mult))
            dve.wait_ge(exps_done, 1)
            dve.wait_ge(par_done, 1)
            decay_arguments(nc.vector, 0)
            dve.wait_ge(sin_half, 2)
            STT(s[14], s[6], 2.0, s[6], ALU.mult, ALU.mult)
            link(STT(s[15], s[6], 2.0, s[7], ALU.mult, ALU.mult))
            STT(s[8], s[13], 1.0, s[14], ALU.add, ALU.mult)
            link(STT(s[16], s[13], 1.0, s[15], ALU.add, ALU.mult))
            link(TT(s[12], s[13], s[8], ALU.subtract))
            TT(s[3], s[17], s[12], ALU.mult)
            TT(s[4], s[10], s[16], ALU.mult)
            TT(s[5], s[17], s[16], ALU.mult)
            link(TT(s[6], s[10], s[12], ALU.mult))
            TT(stack[:, 2, 0:N], s[3], s[4], ALU.subtract)
            TT(stack[:, 2, N:P], s[4], s[3], ALU.subtract)
            TT(stack[:, 3, 0:N], s[5], s[6], ALU.add).then_inc(stack_done, 1)
            STT(stack[:, 3, N:P], s[5], -1.0, s[6], ALU.mult, ALU.subtract).then_inc(stack_done, 1)

            reduce(0)
            dve.wait_ge(par_t, 2)
            nc.vector.tensor_copy(par[:, 2:4], ps_k[:, 1, 2 * C:4 * C].rearrange("p (q h) -> p q h", q=2)
                                  ).then_inc(par_done, 1)
            dve.wait_ge(par_done, 2)

            def factors(j):
                hs = bass.ds(j * QUAD, QUAD)
                dve.wait_ge(wave_done, j * 2 + 2)
                need(dve, k_done, j * 1)
                for n in (1, 2):
                    TT(wave[:, n], wave[:, n], par[:, n + 1, hs].unsqueeze(2).to_broadcast([P, QUAD, RAD]), ALU.mult
                       ).then_inc(maker, 1)
                TT(e1[:], wave[:, 0], mag[:, 0, hs, :], ALU.mult)
                dve.wait_ge(maker, j * MAKER + 5)
                TT(wave[:, 1], wave[:, 1], wave[:, 2], ALU.add).then_inc(sum_done, 1)
                dve.wait_ge(sum_done, j + 1)
                TT(e2[:], wave[:, 1], mag[:, 1, hs, :], ALU.mult).then_inc(e_done, 1)

            def finish_kernels(j):
                dve.wait_ge(k_done, j + 1)
                need(dve, k_stored, j * 16)
                TT(krow[:], ps_k[:, 0, 0:RAD], dplace[:, bass.ds(j, 1), :].rearrange("p j b -> p (j b)"), ALU.add
                   ).then_inc(krow_done, 1)

            def split_x(i, k):
                dve.wait_ge(xh_done, i * PG + (k + 1))
                nc.vector.tensor_tensor(xl[:, k % 2], ps_t[:], xh[:, k % 2], ALU.subtract).then_inc(xl_done, 1)

            dve.wait_ge(mag_done, 1)
            factors(0)
            dve.wait_ge(in_d, 64)
            finish_kernels(0)
            dve.wait_ge(exps_done, 1)
            angles(dve, nc.vector, 1)
            reduce(1)
            split_x(0, 0)
            factors(1)
            finish_kernels(1)

            dve.wait_ge(in_len1, 16)
            nc.vector.tensor_copy(duo_t[:], duo_i[:])
            for n in range(2):
                for g in range(2):
                    TS(limit[g * B:(g + 1) * B, n:n + 1], len1_i[g * B:(g + 1) * B, :], -float(P * (g != n)), None,
                       ALU.add).then_inc(limit_done, 1)

            def tables():
                dve.wait_ge(in_ints, 48)
                nc.vector.tensor_copy(row_t[:], row_i)
                nc.vector.tensor_copy(chan_of[:], chan_i[:])
                nc.vector.tensor_copy(sess_of[:], sess_i[:])
                link(nc.vector.tensor_copy(ints_f[:], ints[:]))
                TS(onehot[:], ints_f[0:SESS, 2, :], sess_of[:], None, ALU.is_equal).then_inc(onehot_done, 1)
                for n in range(2):
                    part = slice(n * C, (n + 1) * C)
                    own = ints_f[part].rearrange("p v (q b) -> p v q b", b=2)
                    nc.vector.tensor_copy(cols[part, :, 3], own[:, 0, :, n])
                    last = TS(cols[part, :, 2], own[:, 1, :, n], chan_of[part, :], None, ALU.is_gt)
                link(last)

            def split_w(i, k):
                dve.wait_ge(wh_done, i * GROUP + (k + 1))
                nc.vector.tensor_tensor(wl[:, k % 4, P:], wf[:, k % GROUP, P:], wh[:, k % 4, P:],
                                        ALU.subtract).then_inc(wl_done, 1)

            def keep_y(i, k):
                need(dve, y_stored[(k // 2) % 2], i * 128 + 64 * (k // 4))
                nc.vector.scalar_tensor_tensor(
                    yst[:, (k // 2) % 2, k % 2].rearrange("p m t -> p (m t)"), duo_t[:].rearrange("p m t -> p (m t)"),
                    limit[:, k % 2:k % 2 + 1], ps_y[:, k % 4, ::-1],
                    ALU.is_lt, ALU.mult).then_inc(y_done, 1)

            def keep_pair(i, k):
                for h in range(2):
                    dve.wait_ge(conv_done, i * GROUP + (2 * k + h + 1))
                    keep_y(i, 2 * k + h)

            for h in range(2):
                split_w(0, h)
            dve.wait_ge(limit_done, 4)

            def body1(i):
                for k in range(PG):
                    j = i * 2 + (k // 2 + AHEAD)
                    if k % 2 == 0 and makes(i):
                        angles(dve, nc.vector, j)
                        reduce(j)
                    if pair_exists(i, k + 1):
                        split_x(i, k + 1)
                    if pair_exists(i, k + 1):
                        split_w(i, 2 * (k + 1))
                    if k % 2 == 0 and makes(i):
                        if isinstance(i, int) and i == 0 and k == 0:
                            dve.wait_ge(mag_done, 2)
                        factors(j)
                    if k % 2 == 1 and makes(i):
                        finish_kernels(j)
                    if pair_exists(i, k + 1):
                        split_w(i, 2 * (k + 1) + 1)
                    keep_pair(i, k)
                    if isinstance(i, int) and i == 0 and k == 0:
                        tables()
                    if isinstance(i, int) and i == 0 and k == 2:
                        dve.wait_ge(bias_mm, 1)
                        nc.vector.tensor_copy(cols[:, :, 0:2], ps_k[:, 1, 0:B].rearrange("p (q b) -> p q b", b=2)
                                              ).then_inc(tables_done, 1)
                        dve.wait_ge(in_ws, 16)
                        nc.vector.tensor_copy(ws_parts[:, :, 0, :], ws).then_inc(ws_upper, 1)
                        dve.wait_ge(ws_upper, 1)
                        nc.vector.tensor_tensor(ws_parts[:, :, 1, :], ws, ws_parts[:, :, 0, :], ALU.subtract
                                                ).then_inc(ws_done, 1)

            bodies_of(dve, body1)
            dve.wait_ge(y_done, C)
            TT(yst[:, 1, 1], yst[:, 1, 1], xin[:, PG - 1, 1], ALU.add).then_inc(last_added, 1)

            def pair_columns(i, k):
                nc.vector.tensor_copy(cols_p[:, k % PG, :], cols[:, bass.ds(i * PG + k, 1), :].rearrange("p q v -> p (q v)")
                                      ).then_inc(cols_done, 1)

            def step(i, k):
                kk = k + LEAD
                if exists(i, k):
                    hf, m = k % 2, (k // 2) % 2
                    half = slice(hf * HALF, (hf + 1) * HALF)
                    dve.wait_ge(mm2_done, i * GROUP + (k + 1))
                    dve.wait_ge(tmask_done, i * GROUP + (k + 1))
                    if hf == 0:
                        need(dve, stored[m], i * 32 + 16 * (k // 4))
                    nc.vector.scalar_tensor_tensor(z[:, m, half], ps_o[:, hf, :], b2_col[:], tmask[:, hf, :],
                                                   ALU.add, ALU.mult).then_inc(z_done, 1)
                if exists(i, kk):
                    m = (kk // 2) % PG
                    dve.wait_ge(xch_done, i * GROUP + (kk + 1))
                    nc.vector.scalar_tensor_tensor(xcl[:, kk % 4, :], xc[:, m, (kk % 2) * HALF:(kk % 2 + 1) * HALF],
                                                   cols_p[:, m, 2:3], xch[:, kk % 4, :], ALU.mult, ALU.subtract
                                                   ).then_inc(xcl_done, 1)
                if exists(i, k + 4) and k % 2 == 0:
                    pair_columns(i, k // 2 + 2)
                if exists(i, k + 1):
                    n = (k + 1) % 2
                    need(dve, z_done, i * GROUP + k)
                    nc.vector.tensor_scalar(tmask[:, n, :], row_t[:, n * HALF:(n + 1) * HALF],
                                            cols_p[:, ((k + 1) // 2) % PG, 3:4], None, ALU.is_lt).then_inc(tmask_done, 1)

            dve.wait_ge(in_late, 48)
            dve.wait_ge(tables_done, 1)
            pair_columns(0, 0)
            dve.wait_ge(cols_done, 1)
            steps_of(dve, step)
            dve.wait_ge(z_done, STEPS)
            TT(z[:, 1, HALF:], z[:, 1, HALF:], xc[:, PG - 1, HALF:], ALU.add).then_inc(last_out, 1)

        @block.tensor
        def _(pe):
            def transpose_x(i, k):
                need(pe, xl_done, i * PG + k)
                pe.wait_ge(x_loaded[k % PG], i * 64 + (64 * (k // PG) + 64))
                for h in range(2):
                    for m in range(DUOS):
                        to = m if h == 0 else DUOS - 1 - m
                        last = nc.tensor.transpose(ps_t[:, h, to * P:(to + 1) * P], xin[:, k % PG, h, m, :], ident[:])
                last.then_inc(xt_done, 1)

            def kernels(j):
                pe.wait_ge(e_done, j + 1)
                need(pe, krow_done, j * 1)
                for q in range(QUAD):
                    last = nc.tensor.matmul(ps_k[RAD * q:RAD * (q + 1), 0, 0:RAD], e2[:, q, :], e1[:, q, :],
                                            start=True, stop=True)
                last.then_inc(k_done, 1)

            pe.wait_ge(ident_done, 2)
            transpose_x(0, 0)
            for n in range(2):
                pe.wait_ge(stack_done, 2 * n + 2)
                if n == 1:
                    pe.wait_ge(par_done, 1)
                for q in (2 * n, 2 * n + 1):
                    last = nc.tensor.transpose(ps_k[:, 1, q * C:(q + 1) * C], stack[:, q, :], ident[0:C, 0:C])
                last.then_inc(par_t, 1)
            kernels(0)
            kernels(1)
            pe.wait_ge(xl_done, 1)
            for _ in range(5):
                nc.tensor.matmul(ps_y[:, 3, :], ident[:], xf[:, 0, 0, :], start=True, stop=True)

            def conv(i, k):
                xs = k % 2
                pe.wait_ge(xl_done, i * PG + (k + 1))
                need(pe, y_done, i * GROUP + (2 * k - 2))
                def lags(w, n, c, duos):
                    own = w[:, n, :].rearrange("p (m v t) -> p m v t", v=2, t=P)
                    return own[:, (c + 1) // 2:(c + 1) // 2 + duos, (c + 1) % 2, :]

                def duo_product(h, c):
                    duos = (CH - c) // 2
                    dst = ps_y[:, 2 * (k % 2) + h, 0:duos * P].rearrange("p (m t) -> p m t", t=P)
                    cols = slice(c * B, (c + 2) * B) if h == 0 else slice((CH - 2 - c) * B, (CH - c) * B)
                    if c >= SPLIT:
                        return nc.tensor.matmul(dst, xf[:, xs, h, cols], lags(wf, 2 * k + h, c, duos),
                                                start=False, stop=(c == CH - 2))
                    for t, (w, v) in enumerate(((wh, xh), (wl, xh), (wh, xl))):
                        last = nc.tensor.matmul(dst, v[:, xs, h, cols], lags(w, (2 * k + h) % 4, c, duos),
                                                start=(c == 0 and t == 0), stop=False)
                    return last

                for h in range(2):
                    pe.wait_ge(wl_done, i * GROUP + (2 * k + h + 1))
                    duo_product(h, 0)
                for h in range(2):
                    first = slice(0, B) if h == 0 else slice((CH - 1) * B, CH * B)
                    nc.tensor.matmul(
                        ps_y[(1 - h) * B:(2 - h) * B, 2 * (k % 2) + h, :].rearrange("p (m t) -> p m t", t=P),
                        xf[:, xs, h, first], lags(wf, 2 * k + h, -1, DUOS), start=False, stop=False)
                for h in range(2):
                    for c in range(1, CH - 1):
                        last = duo_product(h, c)
                    last.then_inc(conv_done, 1)

            def body1(i):
                for k in range(PG):
                    if pair_exists(i, k + 1):
                        transpose_x(i, k + 1)
                    if k % 2 == 1 and makes(i):
                        kernels(i * 2 + (k // 2 + AHEAD))
                    conv(i, k)
                    if isinstance(i, int) and i == 0 and k == 1:
                        pe.wait_ge(onehot_done, 1)
                        pe.wait_ge(in_late, 48)
                        nc.tensor.matmul(ps_k[:, 1, 0:B], bs[:], onehot[:], start=True, stop=True).then_inc(bias_mm, 1)

            bodies_of(pe, body1)

            for _ in range(8):
                nc.tensor.matmul(ps_k[:, 0, :], ident[:], xf[:, 0, 0, :], start=True, stop=True)

            pe.wait_ge(xl_done, PAIRS)
            pe.wait_ge(y_done, C)
            pe.wait_ge(wb_zero, 2)

            def step(i, k):
                if exists(i, k):
                    hf = k % 2
                    pe.wait_ge(hid_done, i * (2 * GROUP) + (2 * k + 2))
                    need(pe, z_done, i * GROUP + (k - 1))
                    for b in range(2):
                        last = nc.tensor.matmul(ps_o[b * C:(b + 1) * C, hf, :], w2_s[:], hid[:, hf, b, :],
                                                start=True, stop=True)
                    last.then_inc(mm2_done, 1)
                if exists(i, k + 2):
                    kk = k + 2
                    hf, m, xs = kk % 2, (kk // 2) % PG, kk % 4
                    pe.wait_ge(xcl_done, i * GROUP + (kk + 1))
                    if hf == 0:
                        pe.wait_ge(wb_loaded[m], i * 32 + (32 * (kk // GROUP) + 32))
                    for b in range(2):
                        for t, (part, v) in enumerate(((0, xch), (0, xcl), (1, xch))):
                            last = nc.tensor.matmul(ps_h[:, hf, b, :], wb[:, m, b, part, :], v[:, xs, :],
                                                    start=(t == 0), stop=(t == 2))
                    last.then_inc(mm1_done, 1)

            steps_of(pe, step)


_INS = ["x", "itok_B_78_3631", "itok_B_0_7", "itok_B_2182_4065", "_lenS", "L0_cond_log_dt", "L0_cond_C",
        "L0_cond_log_A_real", "L0_cond_A_imag", "L0_cond_D", "L1_cond_W_sess", "L1_cond_b_sess", "L1_cond_W2",
        "L1_cond_b2"]


def kernel(**inputs):
    import numpy as np
    import concourse.bacc as bacc
    from concourse.bass_utils import run_bass_kernel_spmd

    nc = bacc.Bacc("TRN2", target_bir_lowering=False, num_devices=1, dynamic_dma_scratch_size=8192)
    arrays, args = {}, []
    for name in _INS:
        a = np.ascontiguousarray(inputs[name])
        arrays[f"in_{name}"] = a
        args.append(nc.dram_tensor(f"in_{name}", a.shape, mybir.dt.from_np(a.dtype), kind="ExternalInput").ap())
    args.append(nc.dram_tensor("out_0", (B, C, T), F32, kind="ExternalOutput").ap())
    x, len1, sid, len2, chans, log_dt, cc, log_a, a_imag, dskip, w_sess, b_sess, w2, b2, out = args
    build_program(nc, x, len1, sid, len2, chans, log_dt, cc, log_a, a_imag, dskip, w_sess, b_sess, w2, b2, out)
    r = run_bass_kernel_spmd(nc, [arrays], core_ids=[0])
    return r.results[0]["out_0"]
```
